# Optimizing a Trainium2 kernel written in Bass

```python
import numpy as np
import jax
import jax.numpy as jnp

def _softmax(x, axis=-1):
    return jax.nn.softmax(x, axis=axis)

def _gelu(x):
    return jax.nn.gelu(x, approximate=True)

def _silu(x):
    return jax.nn.silu(x)

def _sigmoid(x):
    return jax.nn.sigmoid(x)

def _layernorm(x, axis=-1, eps=1e-05):
    m = jnp.mean(x, axis=axis, keepdims=True)
    v = jnp.var(x, axis=axis, keepdims=True)
    return (x - m) / jnp.sqrt(v + eps)

def _scatter_add(tgt, idx, src, axis=0):
    return tgt.at[idx].add(src)

def _segment_sum(src, seg, n):
    return jax.ops.segment_sum(src, seg, n)
kernel_name = 'mk_adj_preln_d4_adj_r2_d02992'

def setup_inputs(seed: int=0):
    np.random.seed(seed)
    _w = jnp.asarray

    def _rec_inputs():
        import jax
        import jax.numpy as jnp
        _gk = jax.random.key(seed)
        x = -0.0005963 + 1.001 * jax.random.normal(jax.random.fold_in(_gk, 1), (128, 64, 384), jnp.float32)
        _w = (1.0 + jnp.arange(64, dtype=jnp.float32)) ** (-0.5)
        _w = _w / _w.mean()
        _pij = jnp.clip(0.0625 * _w[:, None] * _w[None, :], 0.0, 1.0)
        _a = jax.random.uniform(jax.random.fold_in(_gk, 2), (128, 64, 64)) < _pij
        adj = _a
        return (x, adj)
    x, adj = _rec_inputs()

    def _L0_gnn_setup():
        import jax, jax.numpy as jnp
        import numpy as np
        ATT_HEAD = 12
        IN_DIM = 384
        OUT_DIM = IN_DIM // ATT_HEAD
        LEAKY_ALPHA = 0.2
        B, N = (8, 256)
        key = jax.random.key(seed)
        ks = jax.random.split(key, 8)
        feat_in = jax.random.normal(ks[0], (B, N, IN_DIM), dtype=jnp.float32)
        adj = jax.random.randint(ks[1], (B, N, N), 0, 2) > 0
        lim_W = float(np.sqrt(6.0 / (IN_DIM + OUT_DIM)))
        W = jax.random.uniform(ks[2], (ATT_HEAD, IN_DIM, OUT_DIM), minval=-lim_W, maxval=lim_W, dtype=jnp.float32)
        b = jnp.zeros((OUT_DIM,), dtype=jnp.float32)
        lim_w = float(np.sqrt(6.0 / (OUT_DIM + 1)))
        w_src = jax.random.uniform(ks[3], (ATT_HEAD, OUT_DIM, 1), minval=-lim_w, maxval=lim_w, dtype=jnp.float32)
        w_dst = jax.random.uniform(ks[4], (ATT_HEAD, OUT_DIM, 1), minval=-lim_w, maxval=lim_w, dtype=jnp.float32)
        std_H = float(np.sqrt(2.0 / (IN_DIM + IN_DIM)))
        H_w = jax.random.normal(ks[5], (IN_DIM, IN_DIM), dtype=jnp.float32) * std_H
        H_b = jax.random.normal(ks[6], (IN_DIM,), dtype=jnp.float32) * 0.01
        return {'feat_in': feat_in, 'adj': adj, 'W': W, 'b': b, 'w_src': w_src, 'w_dst': w_dst, 'H_w': H_w, 'H_b': H_b}
    _L0_gnn_all = _L0_gnn_setup()
    _L0_gnn_in = {k: v for k, v in _L0_gnn_all.items() if k in ('W', 'b', 'w_src', 'w_dst', 'H_w', 'H_b')}
    del _L0_gnn_all

    def _L1_gnn_setup():
        import jax, jax.numpy as jnp
        import numpy as np
        B, S, H = (4, 1024, 384)
        NUM_HEADS = 6
        HEAD_SIZE = H // NUM_HEADS
        NEG = -9000000000000000.0

        def _heads(x):
            b, s, _ = x.shape
            return x.reshape(b, s, NUM_HEADS, HEAD_SIZE).transpose(0, 2, 1, 3)
        key = jax.random.key(seed)
        ks = jax.random.split(key, 10)
        seq_inputs = jax.random.normal(ks[0], (B, S, H), dtype=jnp.float32)
        gm = jax.random.randint(ks[1], (B, S, S), 0, 2) > 0
        graph_mask = gm | jnp.eye(S, dtype=bool)[None]
        sc = 1.0 / np.sqrt(H)
        Wq = jax.random.normal(ks[2], (H, H), dtype=jnp.float32) * sc
        bq = jnp.zeros((H,), dtype=jnp.float32)
        Wk = jax.random.normal(ks[3], (H, H), dtype=jnp.float32) * sc
        bk = jnp.zeros((H,), dtype=jnp.float32)
        Wv = jax.random.normal(ks[4], (H, H), dtype=jnp.float32) * sc
        bv = jnp.zeros((H,), dtype=jnp.float32)
        Wf = jax.random.normal(ks[5], (H, H), dtype=jnp.float32) * sc
        bf = jnp.zeros((H,), dtype=jnp.float32)
        return {'seq_inputs': seq_inputs, 'Wq': Wq, 'bq': bq, 'Wk': Wk, 'bk': bk, 'Wv': Wv, 'bv': bv, 'Wf': Wf, 'bf': bf, 'graph_mask': graph_mask}
    _L1_gnn_all = _L1_gnn_setup()
    _L1_gnn_in = {k: v for k, v in _L1_gnn_all.items() if k in ('Wq', 'bq', 'Wk', 'bk', 'Wv', 'bv', 'Wf', 'bf')}
    del _L1_gnn_all

    def _L2_gnn_setup():
        import jax, jax.numpy as jnp
        import numpy as np
        ATT_HEAD = 12
        IN_DIM = 384
        OUT_DIM = IN_DIM // ATT_HEAD
        LEAKY_ALPHA = 0.2
        B, N = (8, 256)
        key = jax.random.key(seed)
        ks = jax.random.split(key, 8)
        feat_in = jax.random.normal(ks[0], (B, N, IN_DIM), dtype=jnp.float32)
        adj = jax.random.randint(ks[1], (B, N, N), 0, 2) > 0
        lim_W = float(np.sqrt(6.0 / (IN_DIM + OUT_DIM)))
        W = jax.random.uniform(ks[2], (ATT_HEAD, IN_DIM, OUT_DIM), minval=-lim_W, maxval=lim_W, dtype=jnp.float32)
        b = jnp.zeros((OUT_DIM,), dtype=jnp.float32)
        lim_w = float(np.sqrt(6.0 / (OUT_DIM + 1)))
        w_src = jax.random.uniform(ks[3], (ATT_HEAD, OUT_DIM, 1), minval=-lim_w, maxval=lim_w, dtype=jnp.float32)
        w_dst = jax.random.uniform(ks[4], (ATT_HEAD, OUT_DIM, 1), minval=-lim_w, maxval=lim_w, dtype=jnp.float32)
        std_H = float(np.sqrt(2.0 / (IN_DIM + IN_DIM)))
        H_w = jax.random.normal(ks[5], (IN_DIM, IN_DIM), dtype=jnp.float32) * std_H
        H_b = jax.random.normal(ks[6], (IN_DIM,), dtype=jnp.float32) * 0.01
        return {'feat_in': feat_in, 'adj': adj, 'W': W, 'b': b, 'w_src': w_src, 'w_dst': w_dst, 'H_w': H_w, 'H_b': H_b}
    _L2_gnn_all = _L2_gnn_setup()
    _L2_gnn_in = {k: v for k, v in _L2_gnn_all.items() if k in ('W', 'b', 'w_src', 'w_dst', 'H_w', 'H_b')}
    del _L2_gnn_all

    def _L3_gnn_setup():
        import jax, jax.numpy as jnp
        import numpy as np
        B, S, H = (4, 1024, 384)
        NUM_HEADS = 6
        HEAD_SIZE = H // NUM_HEADS
        NEG = -9000000000000000.0

        def _heads(x):
            b, s, _ = x.shape
            return x.reshape(b, s, NUM_HEADS, HEAD_SIZE).transpose(0, 2, 1, 3)
        key = jax.random.key(seed)
        ks = jax.random.split(key, 10)
        seq_inputs = jax.random.normal(ks[0], (B, S, H), dtype=jnp.float32)
        gm = jax.random.randint(ks[1], (B, S, S), 0, 2) > 0
        graph_mask = gm | jnp.eye(S, dtype=bool)[None]
        sc = 1.0 / np.sqrt(H)
        Wq = jax.random.normal(ks[2], (H, H), dtype=jnp.float32) * sc
        bq = jnp.zeros((H,), dtype=jnp.float32)
        Wk = jax.random.normal(ks[3], (H, H), dtype=jnp.float32) * sc
        bk = jnp.zeros((H,), dtype=jnp.float32)
        Wv = jax.random.normal(ks[4], (H, H), dtype=jnp.float32) * sc
        bv = jnp.zeros((H,), dtype=jnp.float32)
        Wf = jax.random.normal(ks[5], (H, H), dtype=jnp.float32) * sc
        bf = jnp.zeros((H,), dtype=jnp.float32)
        return {'seq_inputs': seq_inputs, 'Wq': Wq, 'bq': bq, 'Wk': Wk, 'bk': bk, 'Wv': Wv, 'bv': bv, 'Wf': Wf, 'bf': bf, 'graph_mask': graph_mask}
    _L3_gnn_all = _L3_gnn_setup()
    _L3_gnn_in = {k: v for k, v in _L3_gnn_all.items() if k in ('Wq', 'bq', 'Wk', 'bk', 'Wv', 'bv', 'Wf', 'bf')}
    del _L3_gnn_all
    return {'x': x, 'adj': adj, 'L0_gnn_W': _L0_gnn_in['W'], 'L0_gnn_b': _L0_gnn_in['b'], 'L0_gnn_w_src': _L0_gnn_in['w_src'], 'L0_gnn_w_dst': _L0_gnn_in['w_dst'], 'L0_gnn_H_w': _L0_gnn_in['H_w'], 'L0_gnn_H_b': _L0_gnn_in['H_b'], 'L1_gnn_Wq': _L1_gnn_in['Wq'], 'L1_gnn_bq': _L1_gnn_in['bq'], 'L1_gnn_Wk': _L1_gnn_in['Wk'], 'L1_gnn_bk': _L1_gnn_in['bk'], 'L1_gnn_Wv': _L1_gnn_in['Wv'], 'L1_gnn_bv': _L1_gnn_in['bv'], 'L1_gnn_Wf': _L1_gnn_in['Wf'], 'L1_gnn_bf': _L1_gnn_in['bf'], 'L2_gnn_W': _L2_gnn_in['W'], 'L2_gnn_b': _L2_gnn_in['b'], 'L2_gnn_w_src': _L2_gnn_in['w_src'], 'L2_gnn_w_dst': _L2_gnn_in['w_dst'], 'L2_gnn_H_w': _L2_gnn_in['H_w'], 'L2_gnn_H_b': _L2_gnn_in['H_b'], 'L3_gnn_Wq': _L3_gnn_in['Wq'], 'L3_gnn_bq': _L3_gnn_in['bq'], 'L3_gnn_Wk': _L3_gnn_in['Wk'], 'L3_gnn_bk': _L3_gnn_in['bk'], 'L3_gnn_Wv': _L3_gnn_in['Wv'], 'L3_gnn_bv': _L3_gnn_in['bv'], 'L3_gnn_Wf': _L3_gnn_in['Wf'], 'L3_gnn_bf': _L3_gnn_in['bf']}

def reference(x, adj, L0_gnn_W, L0_gnn_b, L0_gnn_w_src, L0_gnn_w_dst, L0_gnn_H_w, L0_gnn_H_b, L1_gnn_Wq, L1_gnn_bq, L1_gnn_Wk, L1_gnn_bk, L1_gnn_Wv, L1_gnn_bv, L1_gnn_Wf, L1_gnn_bf, L2_gnn_W, L2_gnn_b, L2_gnn_w_src, L2_gnn_w_dst, L2_gnn_H_w, L2_gnn_H_b, L3_gnn_Wq, L3_gnn_bq, L3_gnn_Wk, L3_gnn_bk, L3_gnn_Wv, L3_gnn_bv, L3_gnn_Wf, L3_gnn_bf):
    import jax
    import jax.numpy as jnp

    def _L0_gnn_ref(feat_in, adj, W, b, w_src, w_dst, H_w, H_b):
        import jax, jax.numpy as jnp
        import numpy as np
        ATT_HEAD = 12
        IN_DIM = 384
        OUT_DIM = IN_DIM // ATT_HEAD
        LEAKY_ALPHA = 0.2
        B, N = (8, 256)
        h = jnp.einsum('bnd,ade->bane', feat_in, W)
        th = jnp.tanh(h)
        attn_src = jnp.einsum('bane,aeo->bano', th, w_src)
        attn_dst = jnp.einsum('bane,aeo->bano', th, w_dst)
        attn = attn_src + jnp.swapaxes(attn_dst, 2, 3)
        attn = jnp.where(attn >= 0, attn, LEAKY_ALPHA * attn)
        mask = ~adj[:, None, :, :]
        attn = jnp.where(mask, jnp.float32(-999.0), attn)
        attn = jax.nn.softmax(attn, axis=-1)
        feat_out = jnp.einsum('banm,bame->bane', attn, h) + b
        feat_out = jnp.swapaxes(feat_out, 1, 2).reshape(feat_in.shape[0], feat_in.shape[1], -1)
        feat_out = jax.nn.elu(feat_out)
        gate = jax.nn.sigmoid(feat_in @ H_w.T + H_b)
        return gate * feat_out + (1.0 - gate) * feat_in

    def _L1_gnn_ref(seq_inputs, Wq, bq, Wk, bk, Wv, bv, Wf, bf, graph_mask):
        import jax, jax.numpy as jnp
        import numpy as np
        B, S, H = (4, 1024, 384)
        NUM_HEADS = 6
        HEAD_SIZE = H // NUM_HEADS
        NEG = -9000000000000000.0

        def _heads(x):
            b, s, _ = x.shape
            return x.reshape(b, s, NUM_HEADS, HEAD_SIZE).transpose(0, 2, 1, 3)
        q = _heads(seq_inputs @ Wq + bq)
        k = _heads(seq_inputs @ Wk + bk)
        v = _heads(seq_inputs @ Wv + bv)
        scores = jnp.einsum('bhqd,bhkd->bhqk', q, k) / np.sqrt(HEAD_SIZE)
        bias = jnp.where(graph_mask, 0.0, NEG)[:, None]
        probs = jax.nn.softmax(scores + bias, axis=-1)
        ctx = jnp.einsum('bhqk,bhkd->bhqd', probs, v)
        ctx = ctx.transpose(0, 2, 1, 3).reshape(seq_inputs.shape[0], seq_inputs.shape[1], H)
        return ctx @ Wf + bf

    def _L2_gnn_ref(feat_in, adj, W, b, w_src, w_dst, H_w, H_b):
        import jax, jax.numpy as jnp
        import numpy as np
        ATT_HEAD = 12
        IN_DIM = 384
        OUT_DIM = IN_DIM // ATT_HEAD
        LEAKY_ALPHA = 0.2
        B, N = (8, 256)
        h = jnp.einsum('bnd,ade->bane', feat_in, W)
        th = jnp.tanh(h)
        attn_src = jnp.einsum('bane,aeo->bano', th, w_src)
        attn_dst = jnp.einsum('bane,aeo->bano', th, w_dst)
        attn = attn_src + jnp.swapaxes(attn_dst, 2, 3)
        attn = jnp.where(attn >= 0, attn, LEAKY_ALPHA * attn)
        mask = ~adj[:, None, :, :]
        attn = jnp.where(mask, jnp.float32(-999.0), attn)
        attn = jax.nn.softmax(attn, axis=-1)
        feat_out = jnp.einsum('banm,bame->bane', attn, h) + b
        feat_out = jnp.swapaxes(feat_out, 1, 2).reshape(feat_in.shape[0], feat_in.shape[1], -1)
        feat_out = jax.nn.elu(feat_out)
        gate = jax.nn.sigmoid(feat_in @ H_w.T + H_b)
        return gate * feat_out + (1.0 - gate) * feat_in

    def _L3_gnn_ref(seq_inputs, Wq, bq, Wk, bk, Wv, bv, Wf, bf, graph_mask):
        import jax, jax.numpy as jnp
        import numpy as np
        B, S, H = (4, 1024, 384)
        NUM_HEADS = 6
        HEAD_SIZE = H // NUM_HEADS
        NEG = -9000000000000000.0

        def _heads(x):
            b, s, _ = x.shape
            return x.reshape(b, s, NUM_HEADS, HEAD_SIZE).transpose(0, 2, 1, 3)
        q = _heads(seq_inputs @ Wq + bq)
        k = _heads(seq_inputs @ Wk + bk)
        v = _heads(seq_inputs @ Wv + bv)
        scores = jnp.einsum('bhqd,bhkd->bhqk', q, k) / np.sqrt(HEAD_SIZE)
        bias = jnp.where(graph_mask, 0.0, NEG)[:, None]
        probs = jax.nn.softmax(scores + bias, axis=-1)
        ctx = jnp.einsum('bhqk,bhkd->bhqd', probs, v)
        ctx = ctx.transpose(0, 2, 1, 3).reshape(seq_inputs.shape[0], seq_inputs.shape[1], H)
        return ctx @ Wf + bf
    h = jnp.maximum(_layernorm(x, axis=-1), 0.0)
    x = x + _L0_gnn_ref(h, adj, L0_gnn_W, L0_gnn_b, L0_gnn_w_src, L0_gnn_w_dst, L0_gnn_H_w, L0_gnn_H_b)
    h = jnp.maximum(_layernorm(x, axis=-1), 0.0)
    x = x + _L1_gnn_ref(h, L1_gnn_Wq, L1_gnn_bq, L1_gnn_Wk, L1_gnn_bk, L1_gnn_Wv, L1_gnn_bv, L1_gnn_Wf, L1_gnn_bf, adj)
    h = jnp.maximum(_layernorm(x, axis=-1), 0.0)
    x = x + _L2_gnn_ref(h, adj, L2_gnn_W, L2_gnn_b, L2_gnn_w_src, L2_gnn_w_dst, L2_gnn_H_w, L2_gnn_H_b)
    h = jnp.maximum(_layernorm(x, axis=-1), 0.0)
    x = x + _L3_gnn_ref(h, L3_gnn_Wq, L3_gnn_bq, L3_gnn_Wk, L3_gnn_bk, L3_gnn_Wv, L3_gnn_bv, L3_gnn_Wf, L3_gnn_bf, adj)
    return x

_drawn_inputs = setup_inputs


def setup_inputs(seed=0):
    import zlib

    import numpy as np

    out = dict(_drawn_inputs(seed))
    spreads = {'L0_gnn_b': (0.0, 0.1),
     'L1_gnn_bq': (0.0, 0.8),
     'L1_gnn_bk': (0.0, 2.0),
     'L1_gnn_bv': (0.0, 0.1),
     'L1_gnn_bf': (0.0, 0.1),
     'L2_gnn_b': (0.0, 0.493),
     'L3_gnn_bq': (0.0, 0.8),
     'L3_gnn_bk': (0.0, 2.0),
     'L3_gnn_bv': (0.0, 0.1),
     'L3_gnn_bf': (0.0, 0.1)}
    factors = {'L0_gnn_w_src': 11.43, 'L0_gnn_H_b': 32.933, 'L2_gnn_w_src': 18.592, 'L2_gnn_H_b': 52.006}
    for name, (base, spread) in spreads.items():
        noise = np.random.default_rng([zlib.crc32(name.encode()), seed]).standard_normal(out[name].shape)
        drawn = base * np.exp(spread * noise) if base else spread * noise
        out[name] = jnp.asarray(drawn.astype(out[name].dtype))
    for name, factor in factors.items():
        out[name] = (out[name] * factor).astype(out[name].dtype)
    return out
```

```python
from contextlib import ExitStack

import concourse.bass as bass
from concourse import mybir

F32 = mybir.dt.float32
F32R = mybir.dt.float32r
BF16 = mybir.dt.bfloat16
U8 = mybir.dt.uint8
ALU = mybir.AluOpType
ACT = mybir.ActivationFunctionType
AX_X = mybir.AxisListType.X

P = 128
D = 384
NC = D // P
S = 64
GH, GE = 12, 32
MH, ME = 6, 64
GP, MP = GH // 2, MH // 2
EPS = 1e-5
LEAKY = 0.2
NOT_ADJ = -999.0
NEG = 9000000000000000.0


def adj_preln_d4(nc: bass.Bass, a, out):
    NT = a["x"].shape[0] // 2
    SLOTS = NT // 2
    x_dram = a["x"].rearrange("(t g) n d -> t (g n) d", g=2)
    adj_dram = a["adj"].rearrange("(t g) n m -> t (g n) m", g=2)
    out_dram = out.rearrange("(t g) n d -> t (g n) d", g=2)

    with ExitStack() as ctx:
        def sb(name, shape, dt=F32):
            return ctx.enter_context(nc.sbuf_tensor(name, shape, dt))

        def psum(name, shape):
            return ctx.enter_context(nc.psum_tensor(name, shape, F32))

        def sem(name):
            return ctx.enter_context(nc.semaphore(name))

        x = sb("x_sb", [P, NT, D])
        adj = sb("adj_sb", [P, NT, S], U8)
        w_raw = sb("w_raw", [P, 4, NC, D])
        w_hi = sb("w_hi", [P, 4, NC, D], F32R)
        w_lo = sb("w_lo", [P, 4, NC, D], F32R)
        ident = sb("ident", [P, P])
        same_graph = sb("same_graph", [P, P], F32R)
        delta = sb("delta", [P, S])
        headmask = sb("headmask", [P, NC, GH])
        minus_half = sb("minus_half", [P, 2])
        w_col = sb("w_col", [P, 2, 2, NC])
        w_sd = sb("w_sd", [P, 2, NC, 2 * GH])
        gat_b = sb("gat_b", [P, 2, GE])
        hb_split = sb("hb_split", [3, 2, D], BF16)
        ones3 = sb("ones3", [3, P], BF16)
        qk_bias = sb("qk_bias", [P, 2, 2, NC])
        stats = sb("stats", [P, 2, 6])
        moments = sb("moments", [P, 2, 2])
        mean_gap = sb("mean_gap", [P, 2])
        gap_sq = sb("gap_sq", [P, 2])
        neg_mean = sb("neg_mean", [P, 2])
        var_part = sb("var_part", [P, 2])
        var_eps = sb("var_eps", [P, 2])
        rstd = sb("rstd", [P, 2])
        ln_shift = sb("ln_shift", [P, 2])
        h = sb("h", [P, 2, D])
        hT_hi = sb("hT_hi", [P, 2 * D], F32R)
        hT_lo = sb("hT_lo", [P, 2 * D], F32R)
        buf_a = sb("buf_a", [P, 2 * D])
        buf_b = sb("buf_b", [P, 2 * D])
        gate_tanh_odd = sb("gate_tanh_odd", [P, D])
        omg = sb("omg", [P, D])
        val = sb("val", [P, 2, 396])
        val_pair = sb("val_pair", [P, 2, 2, 396])
        rhs_hi = sb("rhs_hi", [P, 2 * D], F32R)
        rhs_lo = sb("rhs_lo", [P, 2 * D], F32R)
        src_logit = sb("src_logit", [P, 2, GH])
        dst_hi = sb("dst_hi", [P, GH], F32R)
        dst_lo = sb("dst_lo", [P, GH])
        no_edge = sb("no_edge", [P, 2, S], U8)
        att = sb("att", [P, 2, 2 * D])
        att_top = sb("att_top", [P, 2, GH])
        attT = sb("attT", [P, 2 * D])
        rec = sb("rec", [P, 2, GH])
        u = sb("u", [P, 2, D])
        elu = sb("elu", [P, 2 * D])
        th, thT = buf_a[:, 0:D], buf_a[:, D:2 * D]
        qT = buf_a[:].rearrange("p (c t) -> p c t", c=NC)
        kT = buf_b[:].rearrange("p (c t) -> p c t", c=NC)
        gate = buf_b[:].rearrange("p (u d) -> p u d", u=2)
        hT4_hi, hT4_lo = (t[:].rearrange("p (u c t) -> p u c t", u=2, c=NC) for t in (hT_hi, hT_lo))
        hT2_hi, hT2_lo = (t[:].rearrange("p (c u t) -> p u c t", u=2, c=NC) for t in (hT_hi, hT_lo))
        ctxT_hi, ctxT_lo = (t[:].rearrange("p (u c t) -> p u c t", u=2, c=NC) for t in (rhs_hi, rhs_lo))
        bv, bf = elu[:, 0:D], elu[:, D:2 * D]
        gate_tanh_of = [gate[:, 0, :], gate_tanh_odd[:]]
        mask_add = omg[:, 0:2 * S].rearrange("p (u m) -> p u m", u=2)
        block_raw = u[:, 0, 0:P]
        two = lambda v: v.rearrange("p (i d) -> p i d", i=2)
        hb_part = [two(v) for v in (att[0:3, 0, :], att[0:3, 1, :], attT[0:3, :])]
        hb_bf = [two(v) for v in (buf_a[0:3, 0:D].bitcast(BF16), buf_a[0:3, D:2 * D].bitcast(BF16), buf_b[0:3, 0:D].bitcast(BF16))]
        hb_rows = two(elu[0:3, :])

        ps_t = psum("ps_t", [P, 512])
        ps_h = psum("ps_h", [P, 512])
        ps_g = psum("ps_g", [P, 512])
        ps_s = psum("ps_s", [P, 2, 512])
        ps_f = psum("ps_f", [P, 2, 512])
        ps_o = psum("ps_o", [P, 512])
        qk_bank = [ps_g[:, 0:2 * P], ps_f[:, 1, 0:2 * P]]
        minus_999 = ps_s[:, 0, 511:512]

        x_in = [sem("x_in_even"), sem("x_in_odd")]
        const_in = sem("const_in")
        w_in = sem("w_in")
        bvf_in = sem("bvf_in")
        const_made = sem("const_made")
        w_hi_made, w_lo_made = sem("w_hi_made"), sem("w_lo_made")
        layer_set = sem("layer_set")
        stats_done, moments_done, var_parts_done = sem("stats_done"), sem("moments_done"), sem("var_parts_done")
        var_done, rstd_done, shift_done = sem("var_done"), sem("rstd_done"), sem("shift_done")
        h_done = sem("h_done")
        hT_ps_done, hT_hi_done, hT_lo_done = sem("hT_ps_done"), sem("hT_hi_done"), sem("hT_lo_done")
        hproj_done, gate_ps_done = sem("hproj_done"), sem("gate_ps_done")
        tanh_done, thT_ps_done, thT_done = sem("tanh_done"), sem("thT_ps_done"), sem("thT_done")
        logit_ps_done, logit_done, dst_lo_done = sem("logit_ps_done"), sem("logit_done"), sem("dst_lo_done")
        rhs_done = sem("rhs_done")
        val_done = sem("val_done")
        val_pair_in = [sem("val_pair_in_even"), sem("val_pair_in_odd")]
        s_ps_done = sem("s_ps_done")
        mask_done = sem("mask_done")
        att_sum_done, att_leaky_done, att_masked_done = sem("att_sum_done"), sem("att_leaky_done"), sem("att_masked_done")
        att_top_done, att_shift_done, att_exp_done = sem("att_top_done"), sem("att_shift_done"), sem("att_exp_done")
        attT_ps_done, attT_done = sem("attT_ps_done"), sem("attT_done")
        out_ps_done, rec_done, u_done = sem("out_ps_done"), sem("rec_done"), sem("u_done")
        relu_done, exp_done, elu_done, gated_done = sem("relu_done"), sem("exp_done"), sem("elu_done"), sem("gated_done")
        gate_tanh_done, omg_done, gate_done = sem("gate_tanh_done"), sem("omg_done"), sem("gate_done")
        kept_h_done, x_kept_done = sem("kept_h_done"), sem("x_kept_done")
        qk_ps_done, qk_done = sem("qk_ps_done"), sem("qk_done")
        ctxT_ps_done, ctxT_hi_done, ctxT_lo_done = sem("ctxT_ps_done"), sem("ctxT_hi_done"), sem("ctxT_lo_done")
        v_ps_done, y_ps_done = sem("v_ps_done"), sem("y_ps_done")
        x_done = sem("x_done")
        out_written = sem("out_written")

        N_CONST = 16 * 10
        AHEAD = 2

        def due(count):
            return not isinstance(count, int) or count > 0

        def slots(eng, slot, ahead=1):
            for T in range(-ahead, 2):
                slot(T, T >= 0, T >= 1, True)
            with eng.Fori(2, SLOTS - ahead, 1) as T:
                slot(T, True, True, True)
            for T in range(SLOTS - ahead, SLOTS + 1):
                slot(T, T < SLOTS, True, False)

        block = ctx.enter_context(nc.Block())

        @block.sync
        def _(sp):
            def load_w(layer):
                names = ["W", "H_wT"] if layer % 2 == 0 else ["Wq", "Wk", "Wv", "Wf"]
                for i, n in enumerate(names):
                    w = a[f"L{layer}_gnn_{n}"]
                    if n == "W":
                        for c in range(NC):
                            sp.dma_start(w_raw[:, i, c, :].rearrange("p (a e) -> p a e", a=GH),
                                         w[:, c * P:(c + 1) * P, :].rearrange("a p e -> p a e")).then_inc(w_in, 16)
                    else:
                        sp.dma_start(w_raw[:, i, :, :], w.rearrange("(c p) e -> p c e", p=P)).then_inc(w_in, 16)

            def load_x(T, par):
                k = 2 * T + par
                if due(need := 32 * T):
                    sp.wait_ge(x_in[par], need)
                sp.dma_start(x[:, k, :], x_dram[k]).then_inc(x_in[par], 16)
                sp.dma_start(adj[:, k, :], adj_dram[k]).then_inc(x_in[par], 16)

            def pair_values(layer, par, count):
                w = 6 * 33 if layer % 2 == 0 else 3 * 65
                sp.wait_ge(val_done, count)
                sp.wait_ge(out_ps_done, count)
                for g in range(2):
                    for half in range(2):
                        sp.dma_start(val_pair[64 * half:64 * half + 64, par, g, half * w:half * w + w],
                                     val[64 * g:64 * g + 64, par, half * w:half * w + w]).then_inc(val_pair_in[par], 16)

            def store_x(T, par):
                k = 2 * T + par
                sp.wait_ge(x_done, 3 * NT + k + 1)
                sp.dma_start(out_dram[k], x[:, k, :]).then_inc(out_written, 16)

            for par in range(2):
                load_x(0, par)
            for dst, src in ((ident[:], a["c_ident"]), (block_raw, a["c_block"]), (delta[:], a["c_delta"]),
                             (headmask[:], a["c_headmask"]), (w_col[:], a["w_src_dst"]), (qk_bias[:], a["bq_bk"])):
                sp.dma_start(dst, src).then_inc(const_in, 16)
            load_w(0)
            for i in range(2):
                g = f"L{2 * i}_gnn_"
                sp.dma_start(gat_b[:, i, :], a[g + "b"].partition_broadcast(P)).then_inc(const_in, 16)
            for i in range(2):
                sp.dma_start(hb_part[0][:, i, :], a[f"L{2 * i}_gnn_H_b"].partition_broadcast(3)).then_inc(const_in, 16)

            for layer in range(4):
                sp.wait_ge(layer_set, 2 * layer + 2)
                if layer < 3:
                    sp.wait_ge(w_lo_made, (2, 6, 8)[layer])
                    sp.wait_ge(w_hi_made, (2, 6, 8)[layer])
                    load_w(layer + 1)
                if layer % 2 == 1:
                    for i, n in enumerate(("bv", "bf")):
                        sp.dma_start(elu[:, i * D:(i + 1) * D], a[f"L{layer}_gnn_{n}"].partition_broadcast(P)).then_inc(bvf_in, 16)

                def slot(T, now, before, after, layer=layer):
                    first = layer * NT + 2 * T
                    counts = [first + par + 1 for par in range(2)]
                    if not isinstance(T, int):
                        counts = [nc.sync.snap(c) for c in counts]
                    for par in range(2):
                        if after and layer == 0:
                            load_x(T + 1, par)
                    for par in range(2):
                        if now:
                            pair_values(layer, par, counts[par])
                        if before and layer == 3:
                            store_x(T - 1, par)

                for T in range(0, 1):
                    slot(T, True, False, True)
                with sp.Fori(1, SLOTS - 1, 1) as T:
                    slot(T, True, True, True)
                for T in range(SLOTS - 1, SLOTS + 1):
                    slot(T, T < SLOTS, True, False)
            sp.wait_ge(out_written, 16 * NT)

        @block.tensor
        def _(pe):
            def three_pass(out_ap, stat_hi, stat_lo, mov_hi, mov_lo, more=False):
                for c in range(NC):
                    for i, (s, m) in enumerate(((stat_hi, mov_hi), (stat_hi, mov_lo), (stat_lo, mov_hi))):
                        mm = nc.tensor.matmul(out_ap, s(c), m(c), start=(c == 0 and i == 0),
                                              stop=(c == NC - 1 and i == 2 and not more))
                return mm

            def w(i, part):
                return lambda c: part[:, i, c, :]

            def h_T(layer, T, par):
                k = 2 * T + par
                pe.wait_ge(h_done, layer * NT + k + 1)
                if layer % 2 == 0:
                    if due(need := layer // 2 * NT + k - par):
                        pe.wait_ge(dst_lo_done, need)
                    if due(need := 2 * (layer // 2 * NT + k - par)):
                        pe.wait_ge(logit_done, need)
                else:
                    if due(need := layer // 2 * NT + k - par - 2):
                        pe.wait_ge(ctxT_hi_done, need)
                    if due(need := layer // 2 * NT + k - par - 2):
                        pe.wait_ge(ctxT_lo_done, need)
                if due(need := layer * NT + k):
                    pe.wait_ge(hT_hi_done, need)
                if due(need := layer * NT + k):
                    pe.wait_ge(hT_lo_done, need)
                for c in range(NC):
                    mm = nc.tensor.transpose(ps_t[:, c * P:(c + 1) * P], h[:, par, c * P:(c + 1) * P], ident[:])
                mm.then_inc(hT_ps_done, 1)

            def gat(layer):
                G0, L0 = layer // 2 * NT, layer * NT

                def project(k, par):
                    pe.wait_ge(hT_hi_done, L0 + k + 1)
                    pe.wait_ge(hT_lo_done, L0 + k + 1)
                    if due(need := G0 + k):
                        pe.wait_ge(tanh_done, need)
                    if due(need := L0 + k):
                        pe.wait_ge(val_done, need)
                    three_pass(ps_h[:, 0:D], lambda c: hT4_hi[:, par, c, :], lambda c: hT4_lo[:, par, c, :],
                               w(0, w_hi), w(0, w_lo)).then_inc(hproj_done, 1)

                def gates(k, par):
                    if due(need := G0 + k):
                        pe.wait_ge(gate_tanh_done, need)
                    three_pass(ps_g[:, 0:D], lambda c: hT4_hi[:, par, c, :], lambda c: hT4_lo[:, par, c, :],
                               w(1, w_hi), w(1, w_lo), more=True)
                    nc.tensor.matmul(ps_g[:, 0:D], ones3[:], hb_split[:, layer // 2, :], start=False,
                                     stop=True).then_inc(gate_ps_done, 1)

                def tanh_T(k, par):
                    pe.wait_ge(tanh_done, G0 + k + 1)
                    pe.wait_ge(hT_hi_done, L0 + k + 2 - par)
                    pe.wait_ge(hT_lo_done, L0 + k + 2 - par)
                    if due(need := 2 * (G0 + k)):
                        pe.wait_ge(logit_done, need)
                    if due(need := G0 + k):
                        pe.wait_ge(dst_lo_done, need)
                    for c in range(NC):
                        mm = nc.tensor.transpose(ps_t[:, c * P:(c + 1) * P], th[:, c * P:(c + 1) * P], ident[:])
                    mm.then_inc(thT_ps_done, 1)

                def node_logits(k):
                    pe.wait_ge(thT_done, G0 + k + 1)
                    for c in range(NC):
                        mm = nc.tensor.matmul(ps_t[:, D:D + 2 * GH], thT[:, c * P:(c + 1) * P],
                                              w_sd[:, layer // 2, c, :], start=(c == 0), stop=(c == NC - 1))
                    mm.then_inc(logit_ps_done, 1)

                def spread_dst(k):
                    pe.wait_ge(rhs_done, 2 * (G0 + k + 1))
                    if due(need := G0 + k):
                        pe.wait_ge(att_masked_done, need)
                    for half in range(2):
                        for i, part in enumerate((rhs_hi, rhs_lo)):
                            mm = nc.tensor.matmul(ps_s[:, half, 0:D], same_graph[:], part[:, half * D:(half + 1) * D],
                                                  start=(i == 0), stop=(i == 1))
                    mm.then_inc(s_ps_done, 1)

                def att_T(k, par):
                    pe.wait_ge(att_exp_done, L0 + k + 1)
                    if due(need := L0 + k):
                        pe.wait_ge(attT_done, need)
                    for p in range(GP):
                        mm = nc.tensor.transpose(ps_f[:, p // 3, p % 3 * P:(p % 3 + 1) * P],
                                                 att[:, par, p * P:(p + 1) * P], ident[:])
                    mm.then_inc(attT_ps_done, 1)

                def aggregate(T, k, par):
                    pe.wait_ge(attT_done, L0 + k + 1)
                    pe.wait_ge(val_pair_in[par], 64 * (layer * SLOTS + T + 1))
                    if due(need := L0 + k):
                        pe.wait_ge(u_done, need)
                    vp = val_pair[:, par].rearrange("q g (b p e) -> q g b p e", b=2, p=GP)
                    for g in range(2):
                        for p in range(GP):
                            mm = nc.tensor.matmul(ps_o[64 * g:64 * g + 64, 66 * p:66 * (p + 1)],
                                                  attT[:, p * P + 64 * g:p * P + 64 * g + 64],
                                                  vp[:, g, :, p, :], start=True, stop=True)
                    mm.then_inc(out_ps_done, 1)

                def slot(T, now, before, after):
                    s0, s1, p0, p1 = 2 * T, 2 * T + 1, 2 * T - 2, 2 * T - 1
                    if now:
                        project(s0, 0)
                    if before:
                        spread_dst(p1)
                    if now:
                        tanh_T(s0, 0)
                    if before:
                        att_T(p0, 0)
                    if now:
                        node_logits(s0)
                    if before:
                        aggregate(T - 1, p0, 0)
                    if now:
                        project(s1, 1)
                        gates(s0, 0)
                        spread_dst(s0)
                        tanh_T(s1, 1)
                        node_logits(s1)
                        gates(s1, 1)
                    if before:
                        att_T(p1, 1)
                    if after:
                        h_T(layer, T + 1, 0)
                    if before:
                        aggregate(T - 1, p1, 1)
                    if after:
                        h_T(layer, T + 1, 1)

                slots(pe, slot)

            def mha(layer):
                M0, L0 = layer // 2 * NT, layer * NT

                def project_T(T, i):
                    if i == 0:
                        pe.wait_ge(hT_hi_done, L0 + 2 * T + 2)
                        pe.wait_ge(hT_lo_done, L0 + 2 * T + 2)
                    if due(need := 3 * M0 + 6 * T + i - 1):
                        pe.wait_ge(qk_done, need)
                    mats, c2 = (0, 1)[i // 3], i % 3
                    hi2, lo2 = (t[:].rearrange("p (c t) -> p c t", c=NC) for t in (hT_hi, hT_lo))
                    three_pass(qk_bank[i % 2], lambda c: w_hi[:, mats, c, c2 * P:(c2 + 1) * P],
                               lambda c: w_lo[:, mats, c, c2 * P:(c2 + 1) * P],
                               lambda c: hi2[:, c, :], lambda c: lo2[:, c, :]).then_inc(qk_ps_done, 1)

                def values(k, par):
                    pe.wait_ge(val_done, L0 + k)
                    pe.wait_ge(x_done, L0 + k - 2 - par)
                    if par == 0:
                        pe.wait_ge(qk_done, 3 * M0 + 3 * k + 6)
                    else:
                        pe.wait_ge(att_sum_done, L0 + k)
                    three_pass(ps_h[:, 0:D], lambda c: hT2_hi[:, par, c, :], lambda c: hT2_lo[:, par, c, :],
                               w(2, w_hi), w(2, w_lo)).then_inc(v_ps_done, 1)

                def scores(k, par):
                    for b in range(2):
                        for g in range(2):
                            for c in range(NC):
                                t = par * P + 64 * g
                                mm = nc.tensor.matmul(ps_s[64 * g:64 * g + 64, b, c * S:(c + 1) * S],
                                                      qT[64 * b:64 * b + 64, c, t:t + 64],
                                                      kT[64 * b:64 * b + 64, c, t:t + 64], start=True, stop=True)
                    mm.then_inc(s_ps_done, 1)

                def att_T(k, par):
                    pe.wait_ge(att_exp_done, L0 + k + 1)
                    pe.wait_ge(attT_done, L0 + k)
                    for c in range(NC):
                        mm = nc.tensor.transpose(ps_f[:, 0, c * P:(c + 1) * P], att[:, par, c * P:(c + 1) * P], ident[:])
                    mm.then_inc(attT_ps_done, 1)

                def aggregate(T, k, par):
                    pe.wait_ge(attT_done, L0 + k + 1)
                    pe.wait_ge(val_pair_in[par], 64 * (layer * SLOTS + T + 1))
                    pe.wait_ge(u_done, L0 + k)
                    vp = val_pair[:, par, :, 0:390].rearrange("q g (b p e) -> q g b p e", b=2, p=MP)
                    for g in range(2):
                        for c in range(NC):
                            o = par * D + c * P + 64 * g
                            mm = nc.tensor.matmul(ps_o[64 * g:64 * g + 64, 130 * c:130 * (c + 1)],
                                                  attT[:, o:o + 64], vp[:, g, :, c, :], start=True, stop=True)
                    mm.then_inc(out_ps_done, 1)

                def context_T(k, par):
                    pe.wait_ge(u_done, L0 + k + 1)
                    if due(need := M0 + k):
                        pe.wait_ge(ctxT_hi_done, need)
                    if due(need := M0 + k):
                        pe.wait_ge(ctxT_lo_done, need)
                    for c in range(NC):
                        mm = nc.tensor.transpose(ps_t[:, c * P:(c + 1) * P], u[:, par, c * P:(c + 1) * P], ident[:])
                    mm.then_inc(ctxT_ps_done, 1)

                def project_out(k, par, now):
                    pe.wait_ge(ctxT_hi_done, M0 + k + 1)
                    pe.wait_ge(ctxT_lo_done, M0 + k + 1)
                    pe.wait_ge(x_done, L0 + k)
                    pe.wait_ge(val_done, L0 + (k + 4 - par if now else k + 2 - par))
                    three_pass(ps_h[:, 0:D], lambda c: ctxT_hi[:, par, c, :], lambda c: ctxT_lo[:, par, c, :],
                               w(3, w_hi), w(3, w_lo)).then_inc(y_ps_done, 1)

                def slot(T, now, before, after):
                    s0, s1, p0, p1 = 2 * T, 2 * T + 1, 2 * T - 2, 2 * T - 1
                    if now:
                        for i in range(3):
                            project_T(T, i)
                    if before:
                        aggregate(T - 1, p0, 0)
                    if now:
                        for i in range(3, 6):
                            project_T(T, i)
                    if before:
                        aggregate(T - 1, p1, 1)
                    if now:
                        values(s0, 0)
                    if before:
                        context_T(p0, 0)
                    if now:
                        scores(s0, 0)
                        values(s1, 1)
                    if before:
                        context_T(p1, 1)
                    if now:
                        scores(s1, 1)
                    if after:
                        h_T(layer, T + 1, 0)
                    if before:
                        project_out(p0, 0, now)
                    if now:
                        att_T(s0, 0)
                    if after:
                        h_T(layer, T + 1, 1)
                    if before:
                        project_out(p1, 1, now)
                    if now:
                        att_T(s1, 1)

                slots(pe, slot)

            pe.wait_ge(const_in, N_CONST)
            pe.wait_ge(const_made, N_MADE)
            for layer in range(4):
                if due(need := layer * NT):
                    pe.wait_ge(x_done, need)
                pe.wait_ge(w_hi_made, (2, 6, 8, 12)[layer])
                pe.wait_ge(w_lo_made, (2, 6, 8, 12)[layer])
                (gat if layer % 2 == 0 else mha)(layer)

        @block.scalar
        def _(act):
            def norm_relu(layer, k, par):
                if due(need := layer * NT + k - 1):
                    act.wait_ge(hT_ps_done, need)
                if layer % 2 == 0:
                    if due(need := layer // 2 * NT + k - 1):
                        act.wait_ge(kept_h_done, need)
                    if due(need := layer * NT + k - 1):
                        act.wait_ge(x_kept_done, need)
                act.wait_ge(shift_done, layer * SLOTS + (k - par) // 2 + 1 if isinstance(k, int) else layer * SLOTS + 1 + T_of[0])
                nc.scalar.activation(h[:, par, :], x[:, k, :], ACT.Relu, bias=ln_shift[:, par:par + 1],
                                     scale=rstd[:, par:par + 1]).then_inc(h_done, 1)

            T_of = [None]

            def hT_part(layer, k, par, kk):
                act.wait_ge(hT_ps_done, layer * NT + k + 1)
                if layer % 2 == 0:
                    if due(need := layer // 2 * NT + k - 1):
                        act.wait_ge(gate_ps_done, need)
                else:
                    if due(need := layer // 2 * NT + k - 1):
                        act.wait_ge(v_ps_done, need)
                dst = (hT4_hi if layer % 2 == 0 else hT2_hi)[:, par]
                nc.scalar.activation(dst, ps_t[:, 0:D].rearrange("p (c t) -> p c t", c=NC),
                                     ACT.Copy).then_inc(hT_hi_done, 1)

            def att_exp(layer, k, par, n):
                act.wait_ge(att_shift_done, layer * NT + k + 1)
                nc.scalar.activation(att[:, par, 0:n], att[:, par, 0:n], ACT.Exp).then_inc(att_exp_done, 1)

            def gat(layer):
                G0, L0 = layer // 2 * NT, layer * NT

                def tanh(k):
                    act.wait_ge(hproj_done, G0 + k + 1)
                    if due(need := G0 + k):
                        act.wait_ge(thT_ps_done, need)
                    nc.scalar.activation(th, ps_h[:, 0:D], ACT.Tanh).then_inc(tanh_done, 1)

                def thT_copy(k):
                    act.wait_ge(thT_ps_done, G0 + k + 1)
                    if due(need := G0 + k):
                        act.wait_ge(logit_ps_done, need)
                    nc.scalar.activation(thT, ps_t[:, 0:D], ACT.Copy).then_inc(thT_done, 1)

                def attT_copy(k):
                    act.wait_ge(attT_ps_done, L0 + k + 1)
                    act.wait_ge(out_ps_done, AHEAD + L0 + k)
                    nc.scalar.activation(attT[:].rearrange("p (b t) -> p b t", b=2), ps_f[:, :, 0:D],
                                         ACT.Copy).then_inc(attT_done, 1)

                def elu_exp(k, par):
                    e = elu[:, par * D:(par + 1) * D]
                    act.wait_ge(u_done, L0 + k + 1)
                    if due(need := G0 + k - 1):
                        act.wait_ge(elu_done, need)
                    nc.scalar.activation(e, u[:, par, :], ACT.Relu, scale=-1.0).then_inc(relu_done, 1)
                    act.wait_ge(relu_done, G0 + k + 1)
                    nc.scalar.activation(e, e, ACT.Exp, scale=-1.0).then_inc(exp_done, 1)

                def gate_tanh(k, par):
                    act.wait_ge(gate_ps_done, G0 + k + 1)
                    if due(need := G0 + k - 1):
                        act.wait_ge(gate_done, need)
                    if par == 0:
                        if due(need := G0 + k - 1):
                            act.wait_ge(gated_done, need)
                    nc.scalar.activation(gate_tanh_of[par], ps_g[:, 0:D], ACT.Tanh, scale=0.5).then_inc(gate_tanh_done, 1)
                    if due(need := G0 + k):
                        act.wait_ge(kept_h_done, need)
                    act.wait_ge(gate_tanh_done, G0 + k + 1)
                    nc.scalar.activation(omg[:], gate_tanh_of[par], ACT.Copy, scale=-0.5, bias=0.5).then_inc(omg_done, 1)

                def gate_scale(k, par):
                    act.wait_ge(gate_tanh_done, G0 + k + 1)
                    if due(need := G0 + k - 1):
                        act.wait_ge(gated_done, need)
                    nc.scalar.activation(gate[:, par, :], gate_tanh_of[par], ACT.Copy, scale=0.5,
                                         bias=0.5).then_inc(gate_done, 1)

                def slot(T, now, before, after):
                    T_of[0] = T + 1
                    s0, s1, p0, p1, n0, n1 = 2 * T, 2 * T + 1, 2 * T - 2, 2 * T - 1, 2 * T + 2, 2 * T + 3
                    if before:
                        gate_scale(p1, 1)
                    if now:
                        tanh(s0)
                        thT_copy(s0)
                    if before:
                        attT_copy(p0)
                        elu_exp(p0, 0)
                    if now:
                        tanh(s1)
                    if before:
                        att_exp(layer, p1, 1, 2 * D)
                    if now:
                        gate_tanh(s0, 0)
                        gate_scale(s0, 0)
                        thT_copy(s1)
                    if after:
                        norm_relu(layer, n0, 0)
                    if now:
                        gate_tanh(s1, 1)
                    if before:
                        attT_copy(p1)
                    if after:
                        hT_part(layer, n0, 0, s0)
                        norm_relu(layer, n1, 1)
                    if before:
                        elu_exp(p1, 1)
                    if after:
                        hT_part(layer, n1, 1, s1)
                    if now:
                        att_exp(layer, s0, 0, 2 * D)

                slots(act, slot)

            def mha(layer):
                M0, L0 = layer // 2 * NT, layer * NT

                def qk_copy(T, i):
                    act.wait_ge(qk_ps_done, 3 * M0 + 6 * T + i + 1)
                    if i == 0:
                        act.wait_ge(s_ps_done, L0 + 2 * T)
                    dst = (qT, kT)[i // 3][:, i % 3, :]
                    nc.scalar.activation(dst, qk_bank[i % 2], ACT.Identity,
                                         bias=qk_bias[:, layer // 2, i // 3, i % 3:i % 3 + 1],
                                         scale=ME ** -0.5 if i < 3 else 1.0).then_inc(qk_done, 1)

                def attT_copy(k, par):
                    act.wait_ge(attT_ps_done, L0 + k + 1)
                    act.wait_ge(out_ps_done, AHEAD + L0 + k - 1)
                    nc.scalar.activation(attT[:, par * D:(par + 1) * D], ps_f[:, 0, 0:D], ACT.Copy).then_inc(attT_done, 1)

                def context_hi(k, par):
                    act.wait_ge(ctxT_ps_done, M0 + k + 1)
                    if due(need := M0 + k - 1):
                        act.wait_ge(y_ps_done, need)
                    nc.scalar.activation(ctxT_hi[:, par], ps_t[:, 0:D].rearrange("p (c t) -> p c t", c=NC),
                                         ACT.Copy).then_inc(ctxT_hi_done, 1)

                def slot(T, now, before, after):
                    T_of[0] = T + 1
                    s0, s1, p0, p1, n0, n1 = 2 * T, 2 * T + 1, 2 * T - 2, 2 * T - 1, 2 * T + 2, 2 * T + 3
                    if now:
                        for i in range(6):
                            qk_copy(T, i)
                    if before:
                        context_hi(p0, 0)
                    if after:
                        norm_relu(layer, n0, 0)
                    if before:
                        context_hi(p1, 1)
                    if after:
                        norm_relu(layer, n1, 1)
                        hT_part(layer, n0, 0, s0)
                    if now:
                        att_exp(layer, s0, 0, D)
                        attT_copy(s0, 0)
                    if after:
                        hT_part(layer, n1, 1, s1)
                    if now:
                        att_exp(layer, s1, 1, D)
                        attT_copy(s1, 1)

                slots(act, slot)

            nc.scalar.preload_act_table(ACT.Exp)
            act.wait_ge(const_made, N_MADE)
            for layer in range(4):
                n_w = (2, 4)[layer % 2]
                if due(need := layer * NT):
                    act.wait_ge(x_done, need)
                act.wait_ge(w_in, 16 * (4, 8, 12, 16)[layer])
                for i in range(n_w):
                    nc.scalar.activation(w_hi[:, i], w_raw[:, i], ACT.Copy).then_inc(w_hi_made, 1)
                if layer % 2 == 1:
                    act.wait_ge(layer_set, 2 * layer + 2)
                (gat if layer % 2 == 0 else mha)(layer)

        @block.vector
        def _(dve):
            def coefficients(layer, T):
                for par in range(2):
                    if layer == 0:
                        dve.wait_ge(x_in[par], 32 * (T + 1))
                    if par == 0:
                        if due(need := 2 * (layer * SLOTS + T)):
                            dve.wait_ge(moments_done, need)
                    nc.vector.bn_stats(stats[:, par, :], x[:, 2 * T + par, :]).then_inc(stats_done, 1)
                n = layer * SLOTS + T
                dve.wait_ge(stats_done, 2 * n + 2)
                if due(need := 3 * n):
                    dve.wait_ge(var_parts_done, need)
                nc.vector.tensor_tensor(moments[:], stats[:, :, 1:3], stats[:, :, 4:6], ALU.add).then_inc(moments_done, 1)
                nc.vector.tensor_tensor(mean_gap[:], stats[:, :, 1], stats[:, :, 4], ALU.subtract).then_inc(moments_done, 1)
                dve.wait_ge(moments_done, 2 * n + 2)
                if due(need := n):
                    dve.wait_ge(var_done, need)
                if due(need := n):
                    dve.wait_ge(shift_done, need)
                nc.vector.scalar_tensor_tensor(out=gap_sq[:], in0=mean_gap[:], scalar=0.25, in1=mean_gap[:],
                                               op0=ALU.mult, op1=ALU.mult).then_inc(var_parts_done, 1)
                nc.vector.tensor_scalar(var_part[:], moments[:, :, 1], 1.0 / D, EPS, ALU.mult, ALU.add).then_inc(var_parts_done, 1)
                nc.vector.tensor_scalar(neg_mean[:], moments[:, :, 0], -0.5, None, ALU.mult).then_inc(var_parts_done, 1)
                dve.wait_ge(var_parts_done, 3 * n + 3)
                nc.vector.tensor_tensor(var_eps[:], var_part[:], gap_sq[:], ALU.add).then_inc(var_done, 1)

            def hT_part(layer, k, par):
                dve.wait_ge(hT_hi_done, layer * NT + k + 1)
                i = par if layer % 2 == 0 else par
                dst, hi = ((hT4_lo, hT4_hi) if layer % 2 == 0 else (hT2_lo, hT2_hi))
                nc.vector.tensor_tensor(dst[:, i], ps_t[:, 0:D].rearrange("p (c t) -> p c t", c=NC),
                                        hi[:, i].bitcast(F32), ALU.subtract).then_inc(hT_lo_done, 1)

            def att_max(layer, k, par, nh):
                nc.vector.tensor_reduce(att_top[:, par, 0:nh], att[:, par, 0:nh * S].rearrange("p (a m) -> p a m", a=nh),
                                        AX_X, ALU.max).then_inc(att_top_done, 1)

            def gat(layer):
                G0, L0 = layer // 2 * NT, layer * NT

                def add_bias(k, par):
                    dve.wait_ge(tanh_done, G0 + k + 1)
                    if due(need := 64 * (layer * SLOTS + T_now[0])):
                        dve.wait_ge(val_pair_in[par], need)
                    v = val[:, par, :].rearrange("q (b p e) -> q p b e", b=2, p=GP)
                    nc.vector.tensor_tensor(v[:, :, :, 0:GE], ps_h[:, 0:D].rearrange("q (p b e) -> q p b e", p=GP, b=2),
                                            gat_b[:, layer // 2, :].unsqueeze(1).unsqueeze(1).broadcast_to([P, GP, 2, GE]),
                                            ALU.add).then_inc(val_done, 1)

                def mask(k, par):
                    if due(need := G0 + k - 1):
                        dve.wait_ge(att_masked_done, need)
                    nc.vector.tensor_scalar(no_edge[:, par, :], adj[:, k, :], 0.0, None, ALU.is_equal).then_inc(mask_done, 1)

                def logits(k, par):
                    dve.wait_ge(logit_ps_done, G0 + k + 1)
                    if due(need := L0 + k - 1):
                        dve.wait_ge(att_sum_done, need)
                    if due(need := 2 * (G0 + k)):
                        dve.wait_ge(rhs_done, need)
                    nc.vector.tensor_copy(src_logit[:, par, :], ps_t[:, D:D + GH]).then_inc(logit_done, 1)
                    nc.vector.tensor_copy(dst_hi[:], ps_t[:, D + GH:D + 2 * GH]).then_inc(logit_done, 1)
                    dve.wait_ge(logit_done, 2 * (G0 + k + 1))
                    nc.vector.tensor_tensor(dst_lo[:], ps_t[:, D + GH:D + 2 * GH], dst_hi[:].bitcast(F32),
                                            ALU.subtract).then_inc(dst_lo_done, 1)

                def att_logits(k, par):
                    dve.wait_ge(s_ps_done, L0 + k + 1)
                    if due(need := L0 + k - 1):
                        dve.wait_ge(attT_ps_done, need)
                    a4 = att[:, par, :].rearrange("p (b a m) -> p b a m", b=2, a=GP)
                    nc.vector.tensor_tensor(a4, ps_s[:, :, 0:D].rearrange("p b (a m) -> p b a m", a=GP),
                                            src_logit[:, par, :].rearrange("p (b a) -> p b a", b=2).unsqueeze(3)
                                            .broadcast_to([P, 2, GP, S]), ALU.add).then_inc(att_sum_done, 1)
                    dve.wait_ge(att_sum_done, L0 + k + 1)
                    nc.vector.scalar_tensor_tensor(out=att[:, par, :], in0=att[:, par, :], scalar=LEAKY,
                                                   in1=att[:, par, :], op0=ALU.mult, op1=ALU.max).then_inc(att_leaky_done, 1)

                def att_masked(k, par):
                    a3 = att[:, par, :].rearrange("p (a m) -> p a m", a=GH)
                    nc.vector.copy_predicated(a3, no_edge[:, par, :].unsqueeze(1).broadcast_to([P, GH, S]),
                                              minus_999.unsqueeze(2).broadcast_to([P, GH, S])).then_inc(att_masked_done, 1)
                    dve.wait_ge(att_masked_done, G0 + k + 1)
                    att_max(layer, k, par, GH)

                def normalise(k, par):
                    dve.wait_ge(out_ps_done, AHEAD + L0 + k + 1)
                    if due(need := L0 + k):
                        dve.wait_ge(rec_done, need)
                    v = ps_o[:, 0:GH * 33].rearrange("p (a e) -> p a e", a=GH)
                    nc.vector.reciprocal(rec[:, par, :], v[:, :, GE]).then_inc(rec_done, 1)
                    dve.wait_ge(rec_done, L0 + k + 1)
                    if due(need := G0 + k - 1):
                        dve.wait_ge(gated_done, need)
                    nc.vector.tensor_tensor(u[:, par, :].rearrange("p (a e) -> p a e", a=GH), v[:, :, 0:GE],
                                            rec[:, par, :].unsqueeze(2).broadcast_to([P, GH, GE]), ALU.mult).then_inc(u_done, 1)

                def finish(k, par):
                    dve.wait_ge(exp_done, G0 + k + 1)
                    nc.vector.scalar_tensor_tensor(out=u[:, par, :], in0=u[:, par, :], scalar=0.0,
                                                   in1=elu[:, par * D:(par + 1) * D], op0=ALU.max,
                                                   op1=ALU.add).then_inc(elu_done, 1)
                    dve.wait_ge(elu_done, G0 + k + 1)
                    dve.wait_ge(gate_done, G0 + k + 1)
                    nc.vector.scalar_tensor_tensor(out=u[:, par, :], in0=u[:, par, :], scalar=-1.0,
                                                   in1=gate[:, par, :], op0=ALU.add, op1=ALU.mult).then_inc(gated_done, 1)
                    dve.wait_ge(gated_done, G0 + k + 1)
                    dve.wait_ge(x_kept_done, L0 + k + 1)
                    nc.vector.tensor_tensor(x[:, k, :], x[:, k, :], u[:, par, :], ALU.add).then_inc(x_done, 1)

                def slot(T, now, before, after):
                    T_now[0] = T
                    s0, s1, p0, p1, n0, n1 = 2 * T, 2 * T + 1, 2 * T - 2, 2 * T - 1, 2 * T + 2, 2 * T + 3
                    if after:
                        coefficients(layer, T + 1)
                    if now:
                        add_bias(s0, 0)
                    if before:
                        att_logits(p1, 1)
                    if now:
                        logits(s0, 0)
                        if due(need := G0 + 2 * T):
                            dve.wait_ge(att_leaky_done, need)
                        if due(need := G0 + 2 * T):
                            dve.wait_ge(mask_done, need)
                        mask(s0, 0)
                    elif before:
                        dve.wait_ge(att_leaky_done, G0 + 2 * T)
                        dve.wait_ge(mask_done, G0 + 2 * T)
                    if before:
                        att_masked(p1, 1)
                        normalise(p0, 0)
                    if now:
                        add_bias(s1, 1)
                    if before:
                        finish(p0, 0)
                    if now:
                        att_logits(s0, 0)
                        logits(s1, 1)
                        dve.wait_ge(att_leaky_done, G0 + 2 * T + 1)
                        dve.wait_ge(mask_done, G0 + 2 * T + 1)
                        mask(s1, 1)
                        att_masked(s0, 0)
                    if after:
                        hT_part(layer, n0, 0)
                    if before:
                        normalise(p1, 1)
                    if after:
                        hT_part(layer, n1, 1)
                    if before:
                        finish(p1, 1)

                slots(dve, slot)

            T_now = [None]

            def mha(layer):
                M0, L0 = layer // 2 * NT, layer * NT

                def add_bias(k, par):
                    dve.wait_ge(v_ps_done, M0 + k + 1)
                    dve.wait_ge(val_pair_in[par], 64 * (layer * SLOTS + T_now[0]))
                    v = val[:, par, 0:390].rearrange("q (b c e) -> q c b e", b=2, c=MP)
                    nc.vector.tensor_tensor(v[:, :, :, 0:ME], ps_h[:, 0:D].rearrange("q (c b e) -> q c b e", c=MP, b=2),
                                            bv.rearrange("q (c b e) -> q c b e", c=MP, b=2), ALU.add).then_inc(val_done, 1)

                def mask(k, par):
                    dve.wait_ge(att_sum_done, L0 + k - 1)
                    nc.vector.tensor_scalar(mask_add[:, par, :], adj[:, k, :], -1.0, NEG, ALU.add, ALU.mult).then_inc(mask_done, 1)

                def att_logits(k, par):
                    dve.wait_ge(s_ps_done, L0 + k + 1)
                    dve.wait_ge(attT_ps_done, L0 + k - 1)
                    dve.wait_ge(mask_done, L0 + k + 1)
                    nc.vector.tensor_tensor(att[:, par, 0:D].rearrange("p (c b m) -> p b c m", b=2, c=MP),
                                            ps_s[:, :, 0:MP * S].rearrange("p b (c m) -> p b c m", c=MP),
                                            mask_add[:, par, :].unsqueeze(1).unsqueeze(1).broadcast_to([P, 2, MP, S]),
                                            ALU.add).then_inc(att_sum_done, 1)
                    dve.wait_ge(att_sum_done, L0 + k + 1)
                    att_max(layer, k, par, MH)

                def normalise(k, par):
                    dve.wait_ge(out_ps_done, AHEAD + L0 + k + 1)
                    dve.wait_ge(rec_done, L0 + k)
                    v = ps_o[:, 0:390].rearrange("p (a e) -> p a e", a=MH)
                    nc.vector.reciprocal(rec[:, par, 0:MH], v[:, :, ME]).then_inc(rec_done, 1)
                    dve.wait_ge(rec_done, L0 + k + 1)
                    if due(need := M0 + k - 1):
                        dve.wait_ge(ctxT_ps_done, need)
                    nc.vector.tensor_tensor(u[:, par, :].rearrange("p (a e) -> p a e", a=MH), v[:, :, 0:ME],
                                            rec[:, par, 0:MH].unsqueeze(2).broadcast_to([P, MH, ME]), ALU.mult).then_inc(u_done, 1)

                def context_lo(k, par):
                    dve.wait_ge(ctxT_hi_done, M0 + k + 1)
                    nc.vector.tensor_tensor(ctxT_lo[:, par], ps_t[:, 0:D].rearrange("p (c t) -> p c t", c=NC),
                                            ctxT_hi[:, par].bitcast(F32), ALU.subtract).then_inc(ctxT_lo_done, 1)

                def finish(k, par):
                    dve.wait_ge(y_ps_done, M0 + k + 1)
                    dve.wait_ge(x_kept_done, layer * NT + k + 1)
                    nc.vector.tensor_tensor(x[:, k, :], ps_h[:, 0:D], x[:, k, :], ALU.add).then_inc(x_done, 1)

                def slot(T, now, before, after):
                    T_now[0] = T
                    s0, s1, p0, p1, n0, n1 = 2 * T, 2 * T + 1, 2 * T - 2, 2 * T - 1, 2 * T + 2, 2 * T + 3
                    if after:
                        coefficients(layer, T + 1)
                    if now:
                        mask(s0, 0)
                        mask(s1, 1)
                    if before:
                        normalise(p0, 0)
                        normalise(p1, 1)
                    if now:
                        add_bias(s0, 0)
                    if before:
                        context_lo(p0, 0)
                    if now:
                        att_logits(s0, 0)
                        add_bias(s1, 1)
                    if before:
                        context_lo(p1, 1)
                    if now:
                        att_logits(s1, 1)
                    if after:
                        hT_part(layer, n0, 0)
                    if before:
                        finish(p0, 0)
                    if after:
                        hT_part(layer, n1, 1)
                    if before:
                        finish(p1, 1)

                slots(dve, slot)

            dve.wait_ge(const_in, N_CONST)
            nc.vector.memset(minus_half[:], -0.5).then_inc(const_made, 1)
            nc.vector.memset(gap_sq[:], 0.0).then_inc(out_ps_done, AHEAD)
            nc.vector.memset(minus_999, NOT_ADJ).then_inc(const_made, 1)
            nc.vector.memset(ones3[:], 1.0).then_inc(const_made, 1)
            nc.vector.tensor_copy(same_graph[:], block_raw).then_inc(const_made, 1)
            for i in range(2):
                for j in range(2):
                    nc.vector.tensor_tensor(w_sd[:, i, :, j * GH:(j + 1) * GH], headmask[:],
                                            w_col[:, i, j, :].unsqueeze(2).broadcast_to([P, NC, GH]),
                                            ALU.mult).then_inc(const_made, 1)
                nc.vector.tensor_scalar(qk_bias[:, i, 0, :], qk_bias[:, i, 0, :], ME ** -0.5, None, ALU.mult).then_inc(const_made, 1)
            made = 10
            for i in range(3):
                nc.vector.tensor_copy(hb_bf[i], hb_part[i]).then_inc(const_made, 1)
                made += 1
                dve.wait_ge(const_made, made)
                if i < 2:
                    nc.vector.tensor_tensor(hb_part[i + 1], hb_part[i], hb_bf[i], ALU.subtract).then_inc(const_made, 1)
                    made += 1
                    dve.wait_ge(const_made, made)
            nc.vector.tensor_scalar(hb_rows, hb_bf[0], ident[0:3, 0:1], None, ALU.mult).then_inc(const_made, 1)
            made += 1
            dve.wait_ge(const_made, made)
            nc.vector.scalar_tensor_tensor(out=hb_rows, in0=hb_bf[1], scalar=ident[0:3, 1:2], in1=hb_rows,
                                           op0=ALU.mult, op1=ALU.add).then_inc(const_made, 1)
            made += 1
            dve.wait_ge(const_made, made)
            nc.vector.scalar_tensor_tensor(out=hb_split[:], in0=hb_bf[2], scalar=ident[0:3, 2:3], in1=hb_rows,
                                           op0=ALU.mult, op1=ALU.add).then_inc(const_made, 1)
            made += 1
            assert made == N_MADE
            for layer in range(4):
                n_w = (2, 4)[layer % 2]
                if due(need := layer * NT):
                    dve.wait_ge(x_done, need)
                nc.vector.memset(val_pair[:], 0.0).then_inc(layer_set, 1)
                nc.vector.memset(val[:], 1.0).then_inc(layer_set, 1)
                dve.wait_ge(layer_set, 2 * layer + 2)
                for i in range(n_w):
                    dve.wait_ge(w_hi_made, (0, 2, 6, 8)[layer] + i + 1)
                    nc.vector.tensor_tensor(w_lo[:, i], w_raw[:, i], w_hi[:, i].bitcast(F32), ALU.subtract).then_inc(w_lo_made, 1)
                if layer % 2 == 1:
                    dve.wait_ge(bvf_in, 32 * (layer // 2 + 1))
                (gat if layer % 2 == 0 else mha)(layer)

        @block.gpsimd
        def _(pool):
            def coefficients(layer, T):
                n = layer * SLOTS + T
                pool.wait_ge(var_done, n + 1)
                if due(need := 2 * n):
                    pool.wait_ge(h_done, need)
                nc.gpsimd.tensor_tensor(rstd[:], var_eps[:], minus_half[:], ALU.pow).then_inc(rstd_done, 1)
                pool.wait_ge(rstd_done, n + 1)
                nc.gpsimd.tensor_tensor(ln_shift[:], neg_mean[:], rstd[:], ALU.mult).then_inc(shift_done, 1)

            def shift(layer, k, par, nh):
                pool.wait_ge(att_top_done, layer * NT + k + 1)
                v = att[:, par, 0:nh * S].rearrange("p (a m) -> p a m", a=nh)
                nc.gpsimd.tensor_tensor(v, v, att_top[:, par, 0:nh].unsqueeze(2).broadcast_to([P, nh, S]),
                                        ALU.subtract).then_inc(att_shift_done, 1)

            def gat(layer):
                G0, L0 = layer // 2 * NT, layer * NT

                def dst_diagonal(k):
                    if due(need := L0 + k):
                        pool.wait_ge(s_ps_done, need)
                    pool.wait_ge(dst_lo_done, G0 + k + 1)
                    for dst, part in ((rhs_hi, dst_hi[:].bitcast(F32)), (rhs_lo, dst_lo[:])):
                        nc.gpsimd.tensor_tensor(dst[:].rearrange("p (a m) -> p a m", a=GH),
                                                delta[:].unsqueeze(1).broadcast_to([P, GH, S]),
                                                part.unsqueeze(2).broadcast_to([P, GH, S]), ALU.mult).then_inc(rhs_done, 1)

                def keep_h(k, par):
                    pool.wait_ge(omg_done, G0 + k + 1)
                    pool.wait_ge(hT_ps_done, L0 + k + 1)
                    nc.gpsimd.tensor_tensor(h[:, par, :], h[:, par, :], omg[:], ALU.mult).then_inc(kept_h_done, 1)

                def keep_x(k, par):
                    pool.wait_ge(kept_h_done, G0 + k + 1)
                    nc.gpsimd.tensor_tensor(x[:, k, :], x[:, k, :], h[:, par, :], ALU.add).then_inc(x_kept_done, 1)

                def slot(T, now, before, after):
                    s0, s1, p0, p1 = 2 * T, 2 * T + 1, 2 * T - 2, 2 * T - 1
                    if after:
                        coefficients(layer, T + 1)
                    if now:
                        dst_diagonal(s0)
                    if before:
                        shift(layer, p1, 1, GH)
                    if now:
                        keep_h(s0, 0)
                        keep_x(s0, 0)
                        dst_diagonal(s1)
                        keep_h(s1, 1)
                        keep_x(s1, 1)
                        shift(layer, s0, 0, GH)

                slots(pool, slot)

            def mha(layer):
                def add_bf(k):
                    pool.wait_ge(h_done, layer * NT + k + 1)
                    nc.gpsimd.tensor_tensor(x[:, k, :], x[:, k, :], bf, ALU.add).then_inc(x_kept_done, 1)

                def slot(T, now, before, after):
                    s0, s1 = 2 * T, 2 * T + 1
                    if after:
                        coefficients(layer, T + 1)
                    if now:
                        add_bf(s0)
                        add_bf(s1)
                        shift(layer, s0, 0, MH)
                        shift(layer, s1, 1, MH)

                slots(pool, slot)

            pool.wait_ge(const_made, N_MADE)
            for layer in range(4):
                if due(need := layer * NT):
                    pool.wait_ge(x_done, need)
                if layer % 2 == 1:
                    pool.wait_ge(bvf_in, 32 * (layer // 2 + 1))
                (gat if layer % 2 == 0 else mha)(layer)


N_MADE = 10 + 5 + 3


_GAT = ['W', 'b', 'w_src', 'w_dst', 'H_w', 'H_b']
_MHA = ['Wq', 'bq', 'Wk', 'bk', 'Wv', 'bv', 'Wf', 'bf']


def kernel(**inputs):
    import numpy as _np
    import concourse.bacc as _bacc
    from concourse import mybir as _mybir
    from concourse.bass_utils import run_bass_kernel_spmd as _run

    nc = _bacc.Bacc("TRN2", target_bir_lowering=False, num_devices=1)
    given = {"x": inputs["x"], "adj": inputs["adj"]}
    for layer in range(4):
        for n in (_GAT, _MHA)[layer % 2]:
            given[f"L{layer}_gnn_{n}"] = inputs[f"L{layer}_gnn_{n}"]
        if layer % 2 == 0:
            given[f"L{layer}_gnn_H_wT"] = _np.asarray(given.pop(f"L{layer}_gnn_H_w")).T
    for name, of in (("w_src_dst", ("L{}_gnn_w_src", "L{}_gnn_w_dst")), ("bq_bk", ("L{}_gnn_bq", "L{}_gnn_bk"))):
        first = 0 if name == "w_src_dst" else 1
        cols = [[_np.asarray(given.pop(n.format(layer))).reshape(NC, P) for n in of] for layer in (first, first + 2)]
        given[name] = _np.stack([_np.stack(c) for c in cols]).transpose(3, 0, 1, 2)
    token = _np.arange(P)
    given["c_ident"] = _np.eye(P, dtype=_np.float32)
    given["c_block"] = (token[:, None] // S == token[None, :] // S).astype(_np.float32)
    given["c_delta"] = (token[:, None] % S == _np.arange(S)[None, :]).astype(_np.float32)
    feature = _np.arange(D).reshape(NC, P).T
    given["c_headmask"] = (feature[:, :, None] // GE == _np.arange(GH)[None, None, :]).astype(_np.float32)
    arrays, args = {}, {}
    for name, value in given.items():
        v = _np.ascontiguousarray(value)
        arrays[f"in_{name}"] = v
        args[name] = nc.dram_tensor(f"in_{name}", v.shape, _mybir.dt.from_np(v.dtype), kind="ExternalInput").ap()
    out = nc.dram_tensor("out_0", tuple(given["x"].shape), F32, kind="ExternalOutput").ap()
    adj_preln_d4(nc, args, out)
    r = _run(nc, [arrays], core_ids=[0])
    return r.results[0]["out_0"]
```

```python
from contextlib import ExitStack

import concourse.bass as bass
from concourse import mybir

F32 = mybir.dt.float32
F32R = mybir.dt.float32r
BF16 = mybir.dt.bfloat16
U8 = mybir.dt.uint8
ALU = mybir.AluOpType
ACT = mybir.ActivationFunctionType
AX_X = mybir.AxisListType.X

P = 128
D = 384
NC = D // P
S = 64
GH, GE = 12, 32
MH, ME = 6, 64
GP, MP = GH // 2, MH // 2
EPS = 1e-5
LEAKY = 0.2
PARTS = 3
NOT_ADJ = -999.0
NEG = 9000000000000000.0


def adj_preln_d4(nc: bass.Bass, a, out):
    NT = a["x"].shape[0] // 2
    SLOTS = NT // 2
    x_dram = a["x"].rearrange("(t g) n d -> t (g n) d", g=2)
    adj_dram = a["adj"].rearrange("(t g) n m -> t (g n) m", g=2)
    out_dram = out.rearrange("(t g) n d -> t (g n) d", g=2)

    with ExitStack() as ctx:
        def sb(name, shape, dt=F32):
            return ctx.enter_context(nc.sbuf_tensor(name, shape, dt))

        def psum(name, shape):
            return ctx.enter_context(nc.psum_tensor(name, shape, F32))

        def sem(name):
            return ctx.enter_context(nc.semaphore(name))

        x = sb("x_sb", [P, NT, D])
        adj = sb("adj_sb", [P, NT, S], U8)
        w_landing = sb("w_landing", [P, NC, D])
        w_hi = sb("w_hi", [P, 6, NC, D], F32R)
        w_lo = sb("w_lo", [P, 6, NC, D], F32R)
        ident = sb("ident", [P, P])
        ident_bf = sb("ident_bf", [P, P], BF16)
        row_select = sb("row_select", [P, 2, GH])
        select = sb("select", [P, GH, 2, S], BF16)
        headmask = sb("headmask", [P, NC, GH])
        zeros = sb("zeros", [P, 2, GH])
        minus_half = sb("minus_half", [P, 2])
        w_col = sb("w_col", [P, 2, 2, NC])
        w_sd = sb("w_sd", [P, 2, NC, 2 * GH])
        gat_b = sb("gat_b", [P, 2, GE])
        hb_split = sb("hb_split", [3, 2, D], BF16)
        ones3 = sb("ones3", [3, P], BF16)
        qk_bias = sb("qk_bias", [P, 2, 2, NC])
        stats = sb("stats", [P, 2, 6])
        moments = sb("moments", [P, 2, 2])
        mean_gap = sb("mean_gap", [P, 2])
        gap_sq = sb("gap_sq", [P, 2])
        neg_mean = sb("neg_mean", [P, 2])
        var_part = sb("var_part", [P, 2])
        var_eps = sb("var_eps", [P, 2])
        rstd = sb("rstd", [P, 2])
        ln_shift = sb("ln_shift", [P, 2])
        h = sb("h", [P, 2, D])
        hT_hi = sb("hT_hi", [P, 2 * D], F32R)
        hT_lo = sb("hT_lo", [P, 2 * D], F32R)
        buf_a = sb("buf_a", [P, 2 * D])
        buf_b = sb("buf_b", [P, 2 * D])
        val = sb("val", [P, 2, 396])
        val_pair = sb("val_pair", [P, 2, 2, 396])
        ctxT_hi, ctxT_lo = sb("ctxT_hi", [P, NC, P], F32R), sb("ctxT_lo", [P, NC, P], F32R)
        logit_rest = sb("logit_rest", [P, 2 * GH])
        logit_parts = sb("logit_parts", [P, 2, S], BF16)
        logitT = sb("logitT", [P, P + S], BF16)
        no_edge = sb("no_edge", [P, 2, S], U8)
        att = sb("att", [P, 2, 2 * D])
        att_top = sb("att_top", [P, 2, GH])
        attT = sb("attT", [P, 2 * D])
        rec = sb("rec", [P, 2, GH])
        u = sb("u", [P, 2, D])
        elu = sb("elu", [P, D])
        th, thT = buf_a[:, 0:D], buf_a[:, D:2 * D]
        qT = buf_a[:].rearrange("p (c t) -> p c t", c=NC)
        kT = buf_b[:].rearrange("p (c t) -> p c t", c=NC)
        gate = buf_b[:].rearrange("p (u d) -> p u d", u=2)
        hT4_hi, hT4_lo = (t[:].rearrange("p (u c t) -> p u c t", u=2, c=NC) for t in (hT_hi, hT_lo))
        hT2_hi, hT2_lo = (t[:].rearrange("p (c u t) -> p u c t", u=2, c=NC) for t in (hT_hi, hT_lo))
        part_of = logit_parts[:, :, 0:PARTS * GH].rearrange("p i (t a) -> p i t a", t=PARTS)
        bv, bf = att[:, 0, D:2 * D], att[:, 1, D:2 * D]
        w_second = att[:].rearrange("p u t -> p (u t)")[:, 0:NC * D].rearrange("p (c d) -> p c d", c=NC)
        omg = thT
        mask_add = elu[:, 0:2 * S].rearrange("p (u m) -> p u m", u=2)
        two = lambda v: v.rearrange("p (i d) -> p i d", i=2)
        pair_rows = val_pair[0:3].rearrange("p u g w -> p (u g w)")
        hb_part = [two(v) for v in (pair_rows[:, 0:2 * D], pair_rows[:, 2 * D:4 * D], attT[0:3, :])]
        hb_bf = [two(v) for v in (buf_a[0:3, 0:D].bitcast(BF16), buf_a[0:3, D:2 * D].bitcast(BF16), buf_b[0:3, 0:D].bitcast(BF16))]
        hb_rows = u[0:3]

        ps_t = psum("ps_t", [P, 512])
        ps_h = psum("ps_h", [P, 512])
        ps_g = psum("ps_g", [P, 512])
        ps_s = psum("ps_s", [P, 2, 512])
        ps_f = psum("ps_f", [P, 2, 512])
        ps_o = psum("ps_o", [P, 512])
        qk_bank = [ps_g[:, 0:2 * P], ps_f[:, 1, 0:2 * P]]
        minus_999 = ps_s[:, 0, 511:512]

        x_in = [sem("x_in_even"), sem("x_in_odd")]
        const_in = sem("const_in")
        w_in = [sem("w_in_even"), sem("w_in_odd")]
        bvf_in = sem("bvf_in")
        const_made = sem("const_made")
        w_hi_made, w_lo_made = sem("w_hi_made"), sem("w_lo_made")
        layer_set = sem("layer_set")
        stats_done, moments_done, var_parts_done = sem("stats_done"), sem("moments_done"), sem("var_parts_done")
        var_done, rstd_done, shift_done = sem("var_done"), sem("rstd_done"), sem("shift_done")
        h_done = sem("h_done")
        hT_ps_done, hT_hi_done, hT_lo_done = sem("hT_ps_done"), sem("hT_hi_done"), sem("hT_lo_done")
        hproj_done, gate_ps_done = sem("hproj_done"), sem("gate_ps_done")
        tanh_done, thT_ps_done, thT_done = sem("tanh_done"), sem("thT_ps_done"), sem("thT_done")
        logit_ps_done, part_1_done, rest_done = sem("logit_ps_done"), sem("part_1_done"), sem("rest_done")
        part_2_done, part_3_done = sem("part_2_done"), sem("part_3_done")
        logitT_ps_done, logitT_done = sem("logitT_ps_done"), sem("logitT_done")
        val_done = sem("val_done")
        val_pair_in = [sem("val_pair_in_even"), sem("val_pair_in_odd")]
        s_ps_done = sem("s_ps_done")
        mask_done = sem("mask_done")
        att_scaled_done = sem("att_scaled_done")
        att_sum_done, att_leaky_done, att_masked_done = sem("att_sum_done"), sem("att_leaky_done"), sem("att_masked_done")
        att_top_done, att_shift_done, att_exp_done = sem("att_top_done"), sem("att_shift_done"), sem("att_exp_done")
        attT_ps_done, attT_done = sem("attT_ps_done"), sem("attT_done")
        out_ps_done, rec_done, u_done = sem("out_ps_done"), sem("rec_done"), sem("u_done")
        relu_done, exp_done, elu_done, gated_done = sem("relu_done"), sem("exp_done"), sem("elu_done"), sem("gated_done")
        gate_tanh_done, omg_done, gate_done = sem("gate_tanh_done"), sem("omg_done"), sem("gate_done")
        kept_h_done, x_kept_done = sem("kept_h_done"), sem("x_kept_done")
        qk_ps_done, qk_done = sem("qk_ps_done"), sem("qk_done")
        ctxT_ps_done, ctxT_hi_done, ctxT_lo_done = sem("ctxT_ps_done"), sem("ctxT_hi_done"), sem("ctxT_lo_done")
        v_ps_done, y_ps_done = sem("v_ps_done"), sem("y_ps_done")
        x_done = sem("x_done")
        out_written = sem("out_written")

        N_CONST = 16 * 9
        AHEAD = 2
        W_SPLIT = (2, 6, 8, 12)
        W_FIRST = (0, 2, 0, 2)
        SPLIT_AT = (1, 3, NT - 2, NT)

        def due(count):
            return not isinstance(count, int) or count > 0

        def there(k):
            return not isinstance(k, int) or 0 <= k < NT

        def ahead_of(layer, j):
            return (layer + 1, j - NT) if isinstance(j, int) and j >= NT else (layer, j)

        def slots(eng, slot):
            for T in range(2):
                slot(T)
            with eng.Fori(2, SLOTS - 1, 1) as T:
                slot(T)
            for T in range(SLOTS - 1, SLOTS + 1):
                slot(T)

        def landing(layer, i):
            return w_second if (layer, i) == (0, 1) else w_landing[:]

        def landed(layer, i):
            if i % 2 == 0:
                return 16 * ((0, NC, NC + 2, 2 * NC + 2)[layer] + (NC if layer % 2 == 0 else i // 2 + 1))
            return 16 * ((0, 1, 3, 4)[layer] + i // 2 + 1)

        block = ctx.enter_context(nc.Block())

        @block.sync
        def _(sp):
            def load_w(layer, i):
                n = (("W", "H_wT"), ("Wq", "Wk", "Wv", "Wf"))[layer % 2][i]
                w = a[f"L{layer}_gnn_{n}"]
                to = landing(layer, i)
                if due(need := (0, *W_SPLIT)[layer] + i) and layer > 0:
                    sp.wait_ge(w_lo_made, need)
                    sp.wait_ge(w_hi_made, need)
                if n == "W":
                    for c in range(NC):
                        sp.dma_start(to[:, c, :].rearrange("p (a e) -> p a e", a=GH),
                                     w[:, c * P:(c + 1) * P, :].rearrange("a p e -> p a e")).then_inc(w_in[i % 2], 16)
                else:
                    sp.dma_start(to, w.rearrange("(c p) e -> p c e", p=P)).then_inc(w_in[i % 2], 16)

            def load_x(T, par):
                k = 2 * T + par
                if due(need := 32 * T):
                    sp.wait_ge(x_in[par], need)
                sp.dma_start(x[:, k, :], x_dram[k]).then_inc(x_in[par], 16)
                sp.dma_start(adj[:, k, :], adj_dram[k]).then_inc(x_in[par], 16)

            def pair_values(layer, par, count):
                w = 6 * 33 if layer % 2 == 0 else 3 * 65
                sp.wait_ge(val_done, count)
                sp.wait_ge(out_ps_done, count)
                for g in range(2):
                    for half in range(2):
                        sp.dma_start(val_pair[64 * half:64 * half + 64, par, g, half * w:half * w + w],
                                     val[64 * g:64 * g + 64, par, half * w:half * w + w]).then_inc(val_pair_in[par], 16)

            def store_x(T, par):
                k = 2 * T + par
                sp.wait_ge(x_done, 3 * NT + k + 1)
                sp.dma_start(out_dram[k], x[:, k, :]).then_inc(out_written, 16)

            for T in range(2):
                for par in range(2):
                    load_x(T, par)
            for dst, src in ((ident[:], a["c_ident"]), (row_select[:], a["c_row_select"]),
                             (headmask[:], a["c_headmask"]), (w_col[:], a["w_src_dst"]), (qk_bias[:], a["bq_bk"])):
                sp.dma_start(dst, src).then_inc(const_in, 16)
            load_w(0, 0)
            load_w(0, 1)
            for i in range(2):
                g = f"L{2 * i}_gnn_"
                sp.dma_start(gat_b[:, i, :], a[g + "b"].partition_broadcast(P)).then_inc(const_in, 16)
            for i in range(2):
                sp.dma_start(hb_part[0][:, i, :], a[f"L{2 * i}_gnn_H_b"].partition_broadcast(3)).then_inc(const_in, 16)

            for layer in range(4):
                sp.wait_ge(layer_set, 2 * layer + 2)
                if layer < 3:
                    load_w(layer + 1, 0)
                if layer % 2 == 1:
                    for i, n in enumerate(("bv", "bf")):
                        sp.dma_start((bv, bf)[i], a[f"L{layer}_gnn_{n}"].partition_broadcast(P)).then_inc(bvf_in, 16)

                def slot(T, now, before, after, layer=layer):
                    first = layer * NT + 2 * T
                    counts = [first + par + 1 for par in range(2)]
                    if not isinstance(T, int):
                        counts = [nc.sync.snap(c) for c in counts]
                    for par in range(2):
                        if after and layer == 0:
                            load_x(T + 2, par)
                    for par in range(2):
                        if now:
                            pair_values(layer, par, counts[par])
                        if before and layer == 3:
                            store_x(T - 1, par)

                for T in range(2):
                    slot(T, True, T > 0, True)
                    if layer % 2 == 0 or (layer == 1 and T == 1):
                        load_w(layer + 1, T + 1 if layer % 2 == 0 else 1)
                with sp.Fori(2, SLOTS - 2, 1) as T:
                    slot(T, True, True, True)
                for T in range(SLOTS - 2, SLOTS + 1):
                    slot(T, T < SLOTS, True, False)
                    if layer % 2 == 0 and T == SLOTS - 1:
                        load_w(layer + 1, 3)
            sp.wait_ge(out_written, 16 * NT)

        @block.tensor
        def _(pe):
            def three_pass(out_ap, stat_hi, stat_lo, mov_hi, mov_lo, more=False):
                for c in range(NC):
                    for i, (s, m) in enumerate(((stat_hi, mov_hi), (stat_hi, mov_lo), (stat_lo, mov_hi))):
                        mm = nc.tensor.matmul(out_ap, s(c), m(c), start=(c == 0 and i == 0),
                                              stop=(c == NC - 1 and i == 2 and not more))
                return mm

            def w(i, part):
                return lambda c: part[:, i, c, :]

            def h_T(layer, k, par):
                pe.wait_ge(h_done, layer * NT + k + 1)
                for c in range(NC):
                    mm = nc.tensor.transpose(ps_t[:, c * P:(c + 1) * P], h[:, par, c * P:(c + 1) * P], ident[:])
                mm.then_inc(hT_ps_done, 1)

            def gat(layer):
                G0, L0 = layer // 2 * NT, layer * NT

                def project(k, par):
                    count = 2 if isinstance(k, int) and k == 0 else k + 1
                    pe.wait_ge(hT_hi_done, L0 + count)
                    pe.wait_ge(hT_lo_done, L0 + count)
                    if due(need := G0 + k):
                        pe.wait_ge(logitT_done, need)
                    three_pass(ps_h[:, 0:D], lambda c: hT4_hi[:, par, c, :], lambda c: hT4_lo[:, par, c, :],
                               w(0, w_hi), w(0, w_lo)).then_inc(hproj_done, 1)

                def aggregate(k, par, T):
                    pe.wait_ge(attT_done, L0 + k + 1)
                    pe.wait_ge(val_pair_in[par], 64 * (layer * SLOTS + T))
                    if due(need := L0 + k):
                        pe.wait_ge(u_done, need)
                    vp = val_pair[:, par].rearrange("q g (b p e) -> q g b p e", b=2, p=GP)
                    for g in range(2):
                        for p in range(GP):
                            mm = nc.tensor.matmul(ps_o[64 * g:64 * g + 64, 66 * p:66 * (p + 1)],
                                                  attT[:, p * P + 64 * g:p * P + 64 * g + 64],
                                                  vp[:, g, :, p, :], start=True, stop=True)
                    mm.then_inc(out_ps_done, 1)

                def tanh_T(k):
                    pe.wait_ge(tanh_done, G0 + k + 1)
                    for c in range(NC):
                        mm = nc.tensor.transpose(ps_t[:, c * P:(c + 1) * P], th[:, c * P:(c + 1) * P], ident[:])
                    mm.then_inc(thT_ps_done, 1)

                def gates(k, par):
                    if isinstance(k, int) and k == 0:
                        pe.wait_ge(w_lo_made, W_SPLIT[layer])
                    if due(need := G0 + k):
                        pe.wait_ge(gate_tanh_done, need)
                    three_pass(ps_g[:, 0:D], lambda c: hT4_hi[:, par, c, :], lambda c: hT4_lo[:, par, c, :],
                               w(1, w_hi), w(1, w_lo), more=True)
                    nc.tensor.matmul(ps_g[:, 0:D], ones3[:], hb_split[:, layer // 2, :], start=False,
                                     stop=True).then_inc(gate_ps_done, 1)

                def node_logits(k):
                    pe.wait_ge(thT_done, G0 + k + 1)
                    for c in range(NC):
                        mm = nc.tensor.matmul(ps_t[:, D:D + 2 * GH], thT[:, c * P:(c + 1) * P],
                                              w_sd[:, layer // 2, c, :], start=(c == 0), stop=(c == NC - 1))
                    mm.then_inc(logit_ps_done, 1)

                def logits_T(k):
                    pe.wait_ge(part_3_done, G0 + k + 1)
                    pe.wait_ge(part_2_done, G0 + k + 1)
                    pe.wait_ge(val_done, L0 + k + 1)
                    nc.tensor.matmul(ps_h[:, 0:P], logit_parts[:].rearrange("p i r -> p (i r)"), ident_bf[:],
                                     start=True, stop=True)
                    for g in range(2):
                        t = slice(64 * g, 64 * g + 64)
                        mm = nc.tensor.matmul(ps_h[t, P:P + S], logit_parts[t, 1, :], ident_bf[t, t],
                                              start=True, stop=True)
                    mm.then_inc(logitT_ps_done, 1)

                def att_T(k, par):
                    pe.wait_ge(att_exp_done, L0 + k + 1)
                    if due(need := L0 + k):
                        pe.wait_ge(attT_done, need)
                    for p in range(GP):
                        mm = nc.tensor.transpose(ps_f[:, p // 3, p % 3 * P:(p % 3 + 1) * P],
                                                 att[:, par, p * P:(p + 1) * P], ident[:])
                    mm.then_inc(attT_ps_done, 1)

                def pair_logits(k):
                    pe.wait_ge(logitT_done, G0 + k + 1)
                    if due(need := G0 + k):
                        pe.wait_ge(att_masked_done, need)
                    rows = PARTS * GH
                    for a in range(GH):
                        to = ps_s[:, a // GP, a % GP * S:(a % GP + 1) * S]
                        nc.tensor.matmul(to, logitT[0:rows, 0:P], select[0:rows, a, 0, :], start=True, stop=False)
                        mm = nc.tensor.matmul(to, select[:, a].rearrange("p g m -> p (g m)"), logitT[:, P:P + S],
                                              start=False, stop=True)
                    mm.then_inc(s_ps_done, 1)

                def step(k, par, T):
                    if there(k - 1):
                        logits_T(k - 1)
                    if not isinstance(k, int) or 2 <= k <= NT + 1:
                        if isinstance(k, int) and k == NT + 1:
                            pe.wait_ge(hT_hi_done, L0 + k)
                            pe.wait_ge(hT_lo_done, L0 + k)
                        h_T(*ahead_of(layer, k), par)
                    if there(k - 1):
                        pair_logits(k - 1)
                    if there(k - 2):
                        att_T(k - 2, par)
                    if there(k):
                        project(k, par)
                    if there(k - 2):
                        aggregate(k - 2, par, T)
                    if there(k):
                        tanh_T(k)
                        node_logits(k)
                        gates(k, par)

                def slot(T):
                    step(2 * T, 0, T)
                    step(2 * T + 1, 1, T)

                slots(pe, slot)

            def mha(layer):
                M0, L0 = layer // 2 * NT, layer * NT

                def project_T(T, i):
                    if i == 0:
                        pe.wait_ge(hT_hi_done, L0 + 2 * T + 2)
                        pe.wait_ge(hT_lo_done, L0 + 2 * T + 2)
                    if due(need := 3 * M0 + 6 * T + i - 1):
                        pe.wait_ge(qk_done, need)
                    mats, c2 = 2 + i // 3, i % 3
                    hi2, lo2 = (t[:].rearrange("p (c t) -> p c t", c=NC) for t in (hT_hi, hT_lo))
                    three_pass(qk_bank[i % 2], lambda c: w_hi[:, mats, c, c2 * P:(c2 + 1) * P],
                               lambda c: w_lo[:, mats, c, c2 * P:(c2 + 1) * P],
                               lambda c: hi2[:, c, :], lambda c: lo2[:, c, :]).then_inc(qk_ps_done, 1)

                def values(k, par):
                    pe.wait_ge(val_done, L0 + k)
                    if par == 0:
                        pe.wait_ge(qk_done, 3 * M0 + 3 * k + 6)
                    else:
                        pe.wait_ge(att_sum_done, M0 + k)
                    three_pass(ps_h[:, 0:D], lambda c: hT2_hi[:, par, c, :], lambda c: hT2_lo[:, par, c, :],
                               w(4, w_hi), w(4, w_lo)).then_inc(v_ps_done, 1)

                def scores(k, par):
                    for b in range(2):
                        for g in range(2):
                            for c in range(NC):
                                t = par * P + 64 * g
                                mm = nc.tensor.matmul(ps_s[64 * g:64 * g + 64, b, c * S:(c + 1) * S],
                                                      qT[64 * b:64 * b + 64, c, t:t + 64],
                                                      kT[64 * b:64 * b + 64, c, t:t + 64], start=True, stop=True)
                    mm.then_inc(s_ps_done, 1)

                def att_T(k, par):
                    pe.wait_ge(att_exp_done, L0 + k + 1)
                    pe.wait_ge(attT_done, L0 + k)
                    for c in range(NC):
                        mm = nc.tensor.transpose(ps_f[:, 0, c * P:(c + 1) * P], att[:, par, c * P:(c + 1) * P], ident[:])
                    mm.then_inc(attT_ps_done, 1)

                def aggregate(T, k, par):
                    pe.wait_ge(attT_done, L0 + k + 1)
                    pe.wait_ge(val_pair_in[par], 64 * (layer * SLOTS + T + 1))
                    if par == 1:
                        pe.wait_ge(u_done, L0 + k)
                    elif due(need := k):
                        pe.wait_ge(x_done, L0 + need)
                    vp = val_pair[:, par, :, 0:390].rearrange("q g (b p e) -> q g b p e", b=2, p=MP)
                    for g in range(2):
                        for c in range(NC):
                            o = par * D + c * P + 64 * g
                            mm = nc.tensor.matmul(ps_o[64 * g:64 * g + 64, 130 * c:130 * (c + 1)],
                                                  attT[:, o:o + 64], vp[:, g, :, c, :], start=True, stop=True)
                    mm.then_inc(out_ps_done, 1)

                def context_T(k, par):
                    pe.wait_ge(u_done, L0 + k + 1)
                    if due(need := M0 + k):
                        pe.wait_ge(ctxT_hi_done, need)
                        pe.wait_ge(ctxT_lo_done, need)
                    for c in range(NC):
                        mm = nc.tensor.transpose(ps_t[:, c * P:(c + 1) * P], u[:, par, c * P:(c + 1) * P], ident[:])
                    mm.then_inc(ctxT_ps_done, 1)

                def project_out(k, par):
                    pe.wait_ge(ctxT_hi_done, M0 + k + 1)
                    pe.wait_ge(ctxT_lo_done, M0 + k + 1)
                    if par == 0:
                        pe.wait_ge(u_done, L0 + k + 2)
                    else:
                        pe.wait_ge(x_done, L0 + k)
                    three_pass(ps_o[:, 0:D], lambda c: ctxT_hi[:, c, :], lambda c: ctxT_lo[:, c, :],
                               w(5, w_hi), w(5, w_lo)).then_inc(y_ps_done, 1)

                def slot(T):
                    s0, s1, p0, p1 = 2 * T, 2 * T + 1, 2 * T - 2, 2 * T - 1
                    now, before, after = there(s0), there(p0), there(s0) and (layer < 3 or there(s0 + 2))
                    if now:
                        for i in range(3):
                            project_T(T, i)
                    if before:
                        aggregate(T - 1, p0, 0)
                    if now:
                        for i in range(3, 6):
                            project_T(T, i)
                    if before:
                        aggregate(T - 1, p1, 1)
                    if now:
                        values(s0, 0)
                    if before:
                        context_T(p0, 0)
                    if now:
                        scores(s0, 0)
                        values(s1, 1)
                    if before:
                        project_out(p0, 0)
                        context_T(p1, 1)
                    if now:
                        scores(s1, 1)
                    if after:
                        if before:
                            pe.wait_ge(ctxT_hi_done, M0 + p1 + 1)
                            pe.wait_ge(ctxT_lo_done, M0 + p1 + 1)
                        h_T(*ahead_of(layer, s0 + 2), 0)
                    if now:
                        att_T(s0, 0)
                    if before:
                        project_out(p1, 1)
                    if after:
                        pe.wait_ge(hT_hi_done, L0 + s0 + 3)
                        pe.wait_ge(hT_lo_done, L0 + s0 + 3)
                        h_T(*ahead_of(layer, s1 + 2), 1)
                    if now:
                        att_T(s1, 1)

                slots(pe, slot)

            pe.wait_ge(const_in, N_CONST)
            pe.wait_ge(const_made, N_MADE)
            for par in range(2):
                if par > 0:
                    pe.wait_ge(hT_hi_done, 1)
                    pe.wait_ge(hT_lo_done, 1)
                h_T(0, par, par)
            for layer in range(4):
                if layer > 0:
                    pe.wait_ge(x_done, layer * NT)
                pe.wait_ge(w_lo_made, W_SPLIT[layer] - (1 if layer % 2 == 0 else 0))
                (gat if layer % 2 == 0 else mha)(layer)

        @block.scalar
        def _(act):
            def norm_relu(layer, k, par, T):
                if due(need := layer * NT + k - 1):
                    act.wait_ge(hT_ps_done, need)
                    act.wait_ge(x_kept_done, need)
                act.wait_ge(shift_done, layer * SLOTS + T + 1)
                nc.scalar.activation(h[:, par, :], x[:, k, :], ACT.Relu, bias=ln_shift[:, par:par + 1],
                                     scale=rstd[:, par:par + 1]).then_inc(h_done, 1)

            def hT_part(layer, k, par):
                act.wait_ge(hT_ps_done, layer * NT + k + 1)
                first = isinstance(k, int) and k < 2
                if layer % 2 == (1 if first else 0):
                    if due(need := (layer + 1) // 2 * NT if first else layer // 2 * NT + k - 1):
                        act.wait_ge(gate_ps_done, need)
                elif due(need := layer // 2 * NT if first else layer // 2 * NT + k - 1):
                    act.wait_ge(v_ps_done, need)
                dst = (hT4_hi if layer % 2 == 0 else hT2_hi)[:, par]
                nc.scalar.activation(dst, ps_t[:, 0:D].rearrange("p (c t) -> p c t", c=NC),
                                     ACT.Copy).then_inc(hT_hi_done, 1)

            def weights_hi(layer, i):
                act.wait_ge(w_in[i % 2], landed(layer, i))
                nc.scalar.activation(w_hi[:, W_FIRST[layer] + i], landing(layer, i), ACT.Copy).then_inc(w_hi_made, 1)

            def att_exp(layer, k, par, n):
                act.wait_ge(att_shift_done, layer * NT + k + 1)
                nc.scalar.activation(att[:, par, 0:n], att[:, par, 0:n], ACT.Exp).then_inc(att_exp_done, 1)

            def gat(layer):
                G0, L0 = layer // 2 * NT, layer * NT

                def tanh(k):
                    act.wait_ge(hproj_done, G0 + k + 1)
                    nc.scalar.activation(th, ps_h[:, 0:D], ACT.Tanh).then_inc(tanh_done, 1)

                def thT_copy(k):
                    if due(need := G0 + k):
                        act.wait_ge(kept_h_done, need)
                    act.wait_ge(thT_ps_done, G0 + k + 1)
                    nc.scalar.activation(thT, ps_t[:, 0:D], ACT.Copy).then_inc(thT_done, 1)

                def att_scaled(k, par):
                    act.wait_ge(s_ps_done, L0 + k + 1)
                    if due(need := L0 + k - 1):
                        act.wait_ge(attT_ps_done, need)
                    nc.scalar.activation(att[:, par, :].rearrange("p (b t) -> p b t", b=2), ps_s[:, :, 0:D],
                                         ACT.Copy, scale=LEAKY).then_inc(att_scaled_done, 1)

                def logitT_copy(k):
                    act.wait_ge(logitT_ps_done, G0 + k + 1)
                    if due(need := L0 + k):
                        act.wait_ge(s_ps_done, need)
                    nc.scalar.activation(logitT[:], ps_h[:, 0:P + S], ACT.Copy).then_inc(logitT_done, 1)

                def attT_copy(k):
                    act.wait_ge(attT_ps_done, L0 + k + 1)
                    act.wait_ge(out_ps_done, AHEAD + L0 + k)
                    nc.scalar.activation(attT[:].rearrange("p (b t) -> p b t", b=2), ps_f[:, :, 0:D],
                                         ACT.Copy).then_inc(attT_done, 1)

                def elu_exp(k, par):
                    e = elu[:]
                    act.wait_ge(u_done, L0 + k + 1)
                    if due(need := G0 + k):
                        act.wait_ge(elu_done, need)
                    nc.scalar.activation(e, u[:, par, :], ACT.Relu, scale=-1.0).then_inc(relu_done, 1)
                    act.wait_ge(relu_done, G0 + k + 1)
                    nc.scalar.activation(e, e, ACT.Exp, scale=-1.0).then_inc(exp_done, 1)

                def gate_tanh(k, par):
                    act.wait_ge(gate_ps_done, G0 + k + 1)
                    if due(need := G0 + k - 1):
                        act.wait_ge(gated_done, need)
                    nc.scalar.activation(gate[:, par, :], ps_g[:, 0:D], ACT.Tanh, scale=0.5).then_inc(gate_tanh_done, 1)

                def gate_scale(k, par):
                    act.wait_ge(gate_tanh_done, G0 + k + 1)
                    nc.scalar.activation(omg, gate[:, par, :], ACT.Copy, scale=-0.5, bias=0.5).then_inc(omg_done, 1)
                    act.wait_ge(omg_done, G0 + k + 1)
                    nc.scalar.activation(gate[:, par, :], gate[:, par, :], ACT.Copy, scale=0.5,
                                         bias=0.5).then_inc(gate_done, 1)

                def step(k, par, T):
                    if there(k - 2):
                        attT_copy(k - 2)
                    if there(k):
                        tanh(k)
                        thT_copy(k)
                    after = not isinstance(k, int) or 0 < k <= NT
                    nl, nk = ahead_of(layer, k + 1)
                    if after:
                        norm_relu(nl, nk, 1 - par, 0 if nl > layer else T + par)
                    if there(k - 2):
                        elu_exp(k - 2, par)
                    if there(k - 1):
                        att_exp(layer, k - 1, 1 - par, 2 * D)
                    if there(k):
                        logitT_copy(k)
                    if after:
                        hT_part(nl, nk, 1 - par)
                    if there(k):
                        gate_tanh(k, par)
                        att_scaled(k, par)
                        gate_scale(k, par)
                    if isinstance(k, int) and k in SPLIT_AT:
                        weights_hi(layer + 1, SPLIT_AT.index(k))

                def slot(T):
                    step(2 * T, 0, T)
                    step(2 * T + 1, 1, T)

                slots(act, slot)

            def mha(layer):
                M0, L0 = layer // 2 * NT, layer * NT

                def qk_copy(T, i):
                    act.wait_ge(qk_ps_done, 3 * M0 + 6 * T + i + 1)
                    if i == 0:
                        act.wait_ge(s_ps_done, L0 + 2 * T)
                    dst = (qT, kT)[i // 3][:, i % 3, :]
                    nc.scalar.activation(dst, qk_bank[i % 2], ACT.Identity,
                                         bias=qk_bias[:, layer // 2, i // 3, i % 3:i % 3 + 1],
                                         scale=ME ** -0.5 if i < 3 else 1.0).then_inc(qk_done, 1)

                def attT_copy(k, par):
                    act.wait_ge(attT_ps_done, L0 + k + 1)
                    act.wait_ge(out_ps_done, AHEAD + L0 + k - 1)
                    nc.scalar.activation(attT[:, par * D:(par + 1) * D], ps_f[:, 0, 0:D], ACT.Copy).then_inc(attT_done, 1)

                def context_hi(k):
                    act.wait_ge(ctxT_ps_done, M0 + k + 1)
                    if due(need := M0 + k):
                        act.wait_ge(y_ps_done, need)
                    nc.scalar.activation(ctxT_hi[:], ps_t[:, 0:D].rearrange("p (c t) -> p c t", c=NC),
                                         ACT.Copy).then_inc(ctxT_hi_done, 1)

                def slot(T):
                    s0, s1, p0, p1 = 2 * T, 2 * T + 1, 2 * T - 2, 2 * T - 1
                    now, before, after = there(s0), there(p0), there(s0) and (layer < 3 or there(s0 + 2))
                    (nl, n0), (_, n1) = ahead_of(layer, s0 + 2), ahead_of(layer, s1 + 2)
                    nT = 0 if nl > layer else T + 1
                    if now:
                        for i in range(6):
                            qk_copy(T, i)
                    if before:
                        context_hi(p0)
                    if after:
                        norm_relu(nl, n0, 0, nT)
                    if before:
                        context_hi(p1)
                    if after:
                        norm_relu(nl, n1, 1, nT)
                        hT_part(nl, n0, 0)
                    if now:
                        att_exp(layer, s0, 0, D)
                        attT_copy(s0, 0)
                    if after:
                        hT_part(nl, n1, 1)
                    if now:
                        att_exp(layer, s1, 1, D)
                        attT_copy(s1, 1)
                    if layer < 3 and isinstance(T, int) and T in (1, SLOTS - 1):
                        weights_hi(layer + 1, 0 if T == 1 else 1)

                slots(act, slot)

            nc.scalar.preload_act_table(ACT.Exp)
            for i in range(2):
                weights_hi(0, i)
            norm_relu(0, 0, 0, 0)
            norm_relu(0, 1, 1, 0)
            hT_part(0, 0, 0)
            hT_part(0, 1, 1)
            act.wait_ge(const_made, N_MADE)
            for layer in range(4):
                if layer > 0:
                    act.wait_ge(x_done, layer * NT)
                (gat if layer % 2 == 0 else mha)(layer)

        @block.vector
        def _(dve):
            def coefficients(layer, T):
                if layer > 0 and isinstance(T, int) and T == 0:
                    dve.wait_ge(x_done, (layer - 1) * NT + 2)
                for par in range(2):
                    if layer == 0:
                        dve.wait_ge(x_in[par], 32 * (T + 1))
                    if par == 0:
                        if due(need := 2 * (layer * SLOTS + T)):
                            dve.wait_ge(moments_done, need)
                    nc.vector.bn_stats(stats[:, par, :], x[:, 2 * T + par, :]).then_inc(stats_done, 1)
                n = layer * SLOTS + T
                dve.wait_ge(stats_done, 2 * n + 2)
                if due(need := 3 * n):
                    dve.wait_ge(var_parts_done, need)
                nc.vector.tensor_tensor(moments[:], stats[:, :, 1:3], stats[:, :, 4:6], ALU.add).then_inc(moments_done, 1)
                nc.vector.tensor_tensor(mean_gap[:], stats[:, :, 1], stats[:, :, 4], ALU.subtract).then_inc(moments_done, 1)
                dve.wait_ge(moments_done, 2 * n + 2)
                if due(need := n):
                    dve.wait_ge(var_done, need)
                if due(need := n):
                    dve.wait_ge(shift_done, need)
                nc.vector.scalar_tensor_tensor(out=gap_sq[:], in0=mean_gap[:], scalar=0.25, in1=mean_gap[:],
                                               op0=ALU.mult, op1=ALU.mult).then_inc(var_parts_done, 1)
                nc.vector.tensor_scalar(var_part[:], moments[:, :, 1], 1.0 / D, EPS, ALU.mult, ALU.add).then_inc(var_parts_done, 1)
                nc.vector.tensor_scalar(neg_mean[:], moments[:, :, 0], -0.5, None, ALU.mult).then_inc(var_parts_done, 1)
                dve.wait_ge(var_parts_done, 3 * n + 3)
                nc.vector.tensor_tensor(var_eps[:], var_part[:], gap_sq[:], ALU.add).then_inc(var_done, 1)

            def hT_part(layer, k, par):
                dve.wait_ge(hT_hi_done, layer * NT + k + 1)
                dst, hi = ((hT4_lo, hT4_hi) if layer % 2 == 0 else (hT2_lo, hT2_hi))
                nc.vector.tensor_tensor(dst[:, par], ps_t[:, 0:D].rearrange("p (c t) -> p c t", c=NC),
                                        hi[:, par].bitcast(F32), ALU.subtract).then_inc(hT_lo_done, 1)

            def att_max(layer, k, par, nh):
                nc.vector.tensor_reduce(att_top[:, par, 0:nh], att[:, par, 0:nh * S].rearrange("p (a m) -> p a m", a=nh),
                                        AX_X, ALU.max).then_inc(att_top_done, 1)

            def gat(layer):
                G0, L0 = layer // 2 * NT, layer * NT

                def add_bias(k, par, T):
                    dve.wait_ge(tanh_done, G0 + k + 1)
                    if due(need := 64 * (layer * SLOTS + T)):
                        dve.wait_ge(val_pair_in[par], need)
                    v = val[:, par, :].rearrange("q (b p e) -> q p b e", b=2, p=GP)
                    nc.vector.tensor_tensor(v[:, :, :, 0:GE], ps_h[:, 0:D].rearrange("q (p b e) -> q p b e", p=GP, b=2),
                                            gat_b[:, layer // 2, :].unsqueeze(1).unsqueeze(1).broadcast_to([P, GP, 2, GE]),
                                            ALU.add).then_inc(val_done, 1)

                def mask(k, par):
                    if due(need := G0 + k - 1):
                        dve.wait_ge(att_masked_done, need)
                    nc.vector.tensor_scalar(no_edge[:, par, :], adj[:, k, :], 0.0, None, ALU.is_equal).then_inc(mask_done, 1)

                def logits(k):
                    dve.wait_ge(logit_ps_done, G0 + k + 1)
                    if due(need := G0 + k):
                        dve.wait_ge(logitT_ps_done, need)
                    src_dst = ps_t[:, D:D + 2 * GH].rearrange("p (i a) -> p i a", i=2)
                    nc.vector.tensor_copy(part_of[:, :, 0, :], src_dst).then_inc(part_1_done, 1)
                    dve.wait_ge(part_1_done, G0 + k + 1)
                    nc.vector.tensor_tensor(logit_rest[:].rearrange("p (i a) -> p i a", i=2), src_dst,
                                            part_of[:, :, 0, :], ALU.subtract).then_inc(rest_done, 1)

                def att_leaky(k, par):
                    dve.wait_ge(att_scaled_done, G0 + k + 1)
                    v = att[:, par, :].rearrange("p (b t) -> p b t", b=2)
                    nc.vector.tensor_tensor(v, ps_s[:, :, 0:D], v, ALU.max).then_inc(att_leaky_done, 1)

                def att_masked(k, par):
                    a3 = att[:, par, :].rearrange("p (a m) -> p a m", a=GH)
                    nc.vector.copy_predicated(a3, no_edge[:, par, :].unsqueeze(1).broadcast_to([P, GH, S]),
                                              minus_999.unsqueeze(2).broadcast_to([P, GH, S])).then_inc(att_masked_done, 1)
                def normalise(k, par):
                    dve.wait_ge(out_ps_done, AHEAD + L0 + k + 1)
                    if due(need := L0 + k):
                        dve.wait_ge(rec_done, need)
                    v = ps_o[:, 0:GH * 33].rearrange("p (a e) -> p a e", a=GH)
                    nc.vector.reciprocal(rec[:, par, :], v[:, :, GE]).then_inc(rec_done, 1)
                    dve.wait_ge(rec_done, L0 + k + 1)
                    if due(need := L0 + k - 1):
                        dve.wait_ge(x_done, need)
                    nc.vector.tensor_tensor(u[:, par, :].rearrange("p (a e) -> p a e", a=GH), v[:, :, 0:GE],
                                            rec[:, par, :].unsqueeze(2).broadcast_to([P, GH, GE]), ALU.mult).then_inc(u_done, 1)

                def gated(k, par):
                    dve.wait_ge(exp_done, G0 + k + 1)
                    nc.vector.scalar_tensor_tensor(out=u[:, par, :], in0=u[:, par, :], scalar=0.0,
                                                   in1=elu[:], op0=ALU.max,
                                                   op1=ALU.add).then_inc(elu_done, 1)
                    dve.wait_ge(elu_done, G0 + k + 1)
                    dve.wait_ge(gate_done, G0 + k + 1)
                    nc.vector.scalar_tensor_tensor(out=u[:, par, :], in0=u[:, par, :], scalar=-1.0,
                                                   in1=gate[:, par, :], op0=ALU.add, op1=ALU.mult).then_inc(gated_done, 1)

                def step(k, par, T):
                    if there(k - 1):
                        dve.wait_ge(att_masked_done, G0 + k)
                        att_max(layer, k - 1, 1 - par, GH)
                    if there(k - 2):
                        normalise(k - 2, par)
                    if there(k):
                        add_bias(k, par, T)
                        logits(k)
                    if there(k - 2):
                        gated(k - 2, par)
                    if par == 0 and (not isinstance(T, int) or T < SLOTS):
                        nl, nk = ahead_of(layer, k + 2)
                        coefficients(nl, 0 if nl > layer else T + 1)
                    if not isinstance(k, int) or 0 < k <= NT:
                        hT_part(*ahead_of(layer, k + 1), 1 - par)
                    if isinstance(k, int) and k == 0:
                        mask(0, 0)
                    if there(k):
                        att_leaky(k, par)
                        dve.wait_ge(att_leaky_done, G0 + k + 1)
                        dve.wait_ge(mask_done, L0 + k + 1)
                        if there(k + 1):
                            mask(k + 1, 1 - par)
                        att_masked(k, par)
                    if isinstance(k, int) and k in SPLIT_AT:
                        weights_lo(layer + 1, SPLIT_AT.index(k))

                def slot(T):
                    step(2 * T, 0, T)
                    step(2 * T + 1, 1, T)

                slots(dve, slot)

            def weights_lo(layer, i):
                j = W_FIRST[layer] + i
                dve.wait_ge(w_hi_made, (0, *W_SPLIT)[layer] + i + 1)
                nc.vector.tensor_tensor(w_lo[:, j], landing(layer, i), w_hi[:, j].bitcast(F32),
                                        ALU.subtract).then_inc(w_lo_made, 1)

            def mha(layer):
                M0, L0 = layer // 2 * NT, layer * NT

                def add_bias(k, par, T):
                    dve.wait_ge(v_ps_done, M0 + k + 1)
                    dve.wait_ge(val_pair_in[par], 64 * (layer * SLOTS + T))
                    v = val[:, par, 0:390].rearrange("q (b c e) -> q c b e", b=2, c=MP)
                    nc.vector.tensor_tensor(v[:, :, :, 0:ME], ps_h[:, 0:D].rearrange("q (c b e) -> q c b e", c=MP, b=2),
                                            bv.rearrange("q (c b e) -> q c b e", c=MP, b=2), ALU.add).then_inc(val_done, 1)

                def mask(k, par):
                    if due(need := M0 + k - 1):
                        dve.wait_ge(att_sum_done, need)
                    nc.vector.tensor_scalar(mask_add[:, par, :], adj[:, k, :], -1.0, NEG, ALU.add, ALU.mult).then_inc(mask_done, 1)

                def att_logits(k, par):
                    dve.wait_ge(s_ps_done, L0 + k + 1)
                    dve.wait_ge(attT_ps_done, L0 + k - 1)
                    dve.wait_ge(mask_done, L0 + k + 1)
                    nc.vector.tensor_tensor(att[:, par, 0:D].rearrange("p (c b m) -> p b c m", b=2, c=MP),
                                            ps_s[:, :, 0:MP * S].rearrange("p b (c m) -> p b c m", c=MP),
                                            mask_add[:, par, :].unsqueeze(1).unsqueeze(1).broadcast_to([P, 2, MP, S]),
                                            ALU.add).then_inc(att_sum_done, 1)
                    dve.wait_ge(att_sum_done, M0 + k + 1)
                    att_max(layer, k, par, MH)

                def normalise(k, par):
                    dve.wait_ge(out_ps_done, AHEAD + L0 + k + 1)
                    dve.wait_ge(rec_done, L0 + k)
                    v = ps_o[:, 0:390].rearrange("p (a e) -> p a e", a=MH)
                    nc.vector.reciprocal(rec[:, par, 0:MH], v[:, :, ME]).then_inc(rec_done, 1)
                    dve.wait_ge(rec_done, L0 + k + 1)
                    if due(need := M0 + k - 1):
                        dve.wait_ge(ctxT_ps_done, need)
                    nc.vector.tensor_tensor(u[:, par, :].rearrange("p (a e) -> p a e", a=MH), v[:, :, 0:ME],
                                            rec[:, par, 0:MH].unsqueeze(2).broadcast_to([P, MH, ME]), ALU.mult).then_inc(u_done, 1)

                def context_lo(k):
                    dve.wait_ge(ctxT_hi_done, M0 + k + 1)
                    nc.vector.tensor_tensor(ctxT_lo[:], ps_t[:, 0:D].rearrange("p (c t) -> p c t", c=NC),
                                            ctxT_hi[:].bitcast(F32), ALU.subtract).then_inc(ctxT_lo_done, 1)

                def finish(k):
                    dve.wait_ge(y_ps_done, M0 + k + 1)
                    dve.wait_ge(x_kept_done, L0 + k + 1)
                    nc.vector.tensor_tensor(x[:, k, :], ps_o[:, 0:D], x[:, k, :], ALU.add).then_inc(x_done, 1)

                def slot(T):
                    s0, s1, p0, p1 = 2 * T, 2 * T + 1, 2 * T - 2, 2 * T - 1
                    now, before, after = there(s0), there(p0), there(s0) and (layer < 3 or there(s0 + 2))
                    (nl, n0), (_, n1) = ahead_of(layer, s0 + 2), ahead_of(layer, s1 + 2)
                    if now:
                        mask(s0, 0)
                        mask(s1, 1)
                    if after:
                        coefficients(nl, 0 if nl > layer else T + 1)
                    if before:
                        normalise(p0, 0)
                        normalise(p1, 1)
                    if now:
                        add_bias(s0, 0, T)
                    if before:
                        context_lo(p0)
                    if now:
                        att_logits(s0, 0)
                        add_bias(s1, 1, T)
                    if before:
                        finish(p0)
                        context_lo(p1)
                    if now:
                        att_logits(s1, 1)
                    if after:
                        hT_part(nl, n0, 0)
                    if before:
                        finish(p1)
                    if after:
                        hT_part(nl, n1, 1)
                    if layer < 3 and isinstance(T, int) and T in (1, SLOTS - 1):
                        weights_lo(layer + 1, 0 if T == 1 else 1)

                slots(dve, slot)

            nc.vector.memset(minus_half[:], -0.5).then_inc(const_made, 1)
            coefficients(0, 0)
            for i in range(2):
                weights_lo(0, i)
            dve.wait_ge(const_in, N_CONST)
            nc.vector.memset(zeros[:], 0.0).then_inc(out_ps_done, AHEAD)
            nc.vector.memset(minus_999, NOT_ADJ).then_inc(const_made, 1)
            nc.vector.memset(ones3[:], 1.0).then_inc(const_made, 1)
            nc.vector.memset(logit_parts[:], 0.0).then_inc(const_made, 1)
            nc.vector.tensor_copy(ident_bf[:], ident[:]).then_inc(const_made, 1)
            nc.vector.tensor_copy(select[:], row_select[:].rearrange("p g a -> p a g").unsqueeze(3).broadcast_to([P, GH, 2, S])).then_inc(const_made, 1)
            for i in range(2):
                for j in range(2):
                    nc.vector.tensor_tensor(w_sd[:, i, :, j * GH:(j + 1) * GH], headmask[:],
                                            w_col[:, i, j, :].unsqueeze(2).broadcast_to([P, NC, GH]),
                                            ALU.mult).then_inc(const_made, 1)
                nc.vector.tensor_scalar(qk_bias[:, i, 0, :], qk_bias[:, i, 0, :], ME ** -0.5, None, ALU.mult).then_inc(const_made, 1)
            made = 12
            for i in range(3):
                nc.vector.tensor_copy(hb_bf[i], hb_part[i]).then_inc(const_made, 1)
                made += 1
                dve.wait_ge(const_made, made)
                if i < 2:
                    nc.vector.tensor_tensor(hb_part[i + 1], hb_part[i], hb_bf[i], ALU.subtract).then_inc(const_made, 1)
                    made += 1
                    dve.wait_ge(const_made, made)
            nc.vector.tensor_scalar(hb_rows, hb_bf[0], ident[0:3, 0:1], None, ALU.mult).then_inc(const_made, 1)
            made += 1
            dve.wait_ge(const_made, made)
            nc.vector.scalar_tensor_tensor(out=hb_rows, in0=hb_bf[1], scalar=ident[0:3, 1:2], in1=hb_rows,
                                           op0=ALU.mult, op1=ALU.add).then_inc(const_made, 1)
            made += 1
            dve.wait_ge(const_made, made)
            nc.vector.scalar_tensor_tensor(out=hb_split[:], in0=hb_bf[2], scalar=ident[0:3, 2:3], in1=hb_rows,
                                           op0=ALU.mult, op1=ALU.add).then_inc(const_made, 1)
            made += 1
            assert made == N_MADE
            hT_part(0, 0, 0)
            hT_part(0, 1, 1)
            for layer in range(4):
                if layer > 0:
                    dve.wait_ge(x_done, layer * NT)
                dve.wait_ge(layer_set, 2 * layer + 2)
                if layer % 2 == 1:
                    dve.wait_ge(bvf_in, 32 * (layer // 2 + 1))
                (gat if layer % 2 == 0 else mha)(layer)

        @block.gpsimd
        def _(pool):
            def coefficients(layer, T):
                n = layer * SLOTS + T
                pool.wait_ge(var_done, n + 1)
                if due(need := 2 * n):
                    pool.wait_ge(h_done, need)
                nc.gpsimd.tensor_tensor(rstd[:], var_eps[:], minus_half[:], ALU.pow).then_inc(rstd_done, 1)
                pool.wait_ge(rstd_done, n + 1)
                nc.gpsimd.tensor_tensor(ln_shift[:], neg_mean[:], rstd[:], ALU.mult).then_inc(shift_done, 1)

            def shift(layer, k, par, nh):
                pool.wait_ge(att_top_done, layer * NT + k + 1)
                v = att[:, par, 0:nh * S].rearrange("p (a m) -> p a m", a=nh)
                nc.gpsimd.tensor_tensor(v, v, att_top[:, par, 0:nh].unsqueeze(2).broadcast_to([P, nh, S]),
                                        ALU.subtract).then_inc(att_shift_done, 1)

            def gat(layer):
                G0, L0 = layer // 2 * NT, layer * NT

                def keep_h(k, par):
                    pool.wait_ge(omg_done, G0 + k + 1)
                    pool.wait_ge(hT_ps_done, L0 + k + 1)
                    nc.gpsimd.tensor_tensor(h[:, par, :], h[:, par, :], omg, ALU.mult).then_inc(kept_h_done, 1)
                    pool.wait_ge(kept_h_done, G0 + k + 1)
                    nc.gpsimd.tensor_tensor(x[:, k, :], x[:, k, :], h[:, par, :], ALU.add).then_inc(x_kept_done, 1)

                def parts(k):
                    pool.wait_ge(rest_done, G0 + k + 1)
                    rest = logit_rest[:].rearrange("p (i a) -> p i a", i=2)
                    nc.gpsimd.tensor_tensor(part_of[:, :, 1, :], rest, zeros[:], ALU.add).then_inc(part_2_done, 1)
                    pool.wait_ge(part_2_done, G0 + k + 1)
                    nc.gpsimd.tensor_tensor(part_of[:, :, 2, :], rest, part_of[:, :, 1, :],
                                            ALU.subtract).then_inc(part_3_done, 1)

                def finish(k, par, half):
                    pool.wait_ge(gated_done, G0 + k + 1)
                    xk = x[:].rearrange("p (t s) d -> p t s d", s=2)[:, half, par, :]
                    nc.gpsimd.tensor_tensor(xk, xk, u[:, par, :], ALU.add).then_inc(x_done, 1)

                def step(k, par, T):
                    if there(k - 3):
                        finish(k - 3, 1 - par, T - 2 + par)
                    if par == 1 and (not isinstance(T, int) or T < SLOTS):
                        nl, nk = ahead_of(layer, k + 1)
                        coefficients(nl, 0 if nl > layer else T + 1)
                    if there(k - 1):
                        keep_h(k - 1, 1 - par)
                        shift(layer, k - 1, 1 - par, GH)
                    if due(need := L0 + min(k - 1, NT) if isinstance(k, int) else L0 + k - 1):
                        pool.wait_ge(x_kept_done, need)
                    if there(k):
                        parts(k)

                def slot(T):
                    step(2 * T, 0, T)
                    step(2 * T + 1, 1, T)

                slots(pool, slot)
                finish(NT - 1, 1, SLOTS - 1)

            def mha(layer):
                def add_bf(k):
                    pool.wait_ge(h_done, layer * NT + k + 1)
                    nc.gpsimd.tensor_tensor(x[:, k, :], x[:, k, :], bf, ALU.add).then_inc(x_kept_done, 1)

                def slot(T):
                    s0, s1 = 2 * T, 2 * T + 1
                    if there(s0) and (layer < 3 or there(s0 + 2)):
                        nl, _ = ahead_of(layer, s0 + 2)
                        coefficients(nl, 0 if nl > layer else T + 1)
                    if there(s0):
                        add_bf(s0)
                        add_bf(s1)
                        shift(layer, s0, 0, MH)
                        shift(layer, s1, 1, MH)

                slots(pool, slot)

            pool.wait_ge(const_made, 1)
            coefficients(0, 0)
            for layer in range(4):
                if layer > 0:
                    pool.wait_ge(x_done, layer * NT)
                else:
                    pool.wait_ge(const_made, N_MADE)
                nc.gpsimd.memset(val[:], 1.0).then_inc(layer_set, 1)
                nc.gpsimd.memset(val_pair[:], 0.0).then_inc(layer_set, 1)
                if layer % 2 == 1:
                    pool.wait_ge(bvf_in, 32 * (layer // 2 + 1))
                (gat if layer % 2 == 0 else mha)(layer)


N_MADE = 12 + 5 + 3


_GAT = ['W', 'b', 'w_src', 'w_dst', 'H_w', 'H_b']
_MHA = ['Wq', 'bq', 'Wk', 'bk', 'Wv', 'bv', 'Wf', 'bf']


def kernel(**inputs):
    import numpy as _np
    import concourse.bacc as _bacc
    from concourse import mybir as _mybir
    from concourse.bass_utils import run_bass_kernel_spmd as _run

    nc = _bacc.Bacc("TRN2", target_bir_lowering=False, num_devices=1)
    given = {"x": inputs["x"], "adj": inputs["adj"]}
    for layer in range(4):
        for n in (_GAT, _MHA)[layer % 2]:
            given[f"L{layer}_gnn_{n}"] = inputs[f"L{layer}_gnn_{n}"]
        if layer % 2 == 0:
            given[f"L{layer}_gnn_H_wT"] = _np.asarray(given.pop(f"L{layer}_gnn_H_w")).T
    for name, of in (("w_src_dst", ("L{}_gnn_w_src", "L{}_gnn_w_dst")), ("bq_bk", ("L{}_gnn_bq", "L{}_gnn_bk"))):
        first = 0 if name == "w_src_dst" else 1
        cols = [[_np.asarray(given.pop(n.format(layer))).reshape(NC, P) for n in of] for layer in (first, first + 2)]
        given[name] = _np.stack([_np.stack(c) for c in cols]).transpose(3, 0, 1, 2)
    given["c_ident"] = _np.eye(P, dtype=_np.float32)
    c = _np.zeros((2, S, 2, GH), dtype=_np.float32)
    for g in range(2):
        c[g, :PARTS * GH, g] = _np.tile(_np.eye(GH), (PARTS, 1))
    given["c_row_select"] = c.reshape(P, 2, GH)
    feature = _np.arange(D).reshape(NC, P).T
    given["c_headmask"] = (feature[:, :, None] // GE == _np.arange(GH)[None, None, :]).astype(_np.float32)
    arrays, args = {}, {}
    for name, value in given.items():
        v = _np.ascontiguousarray(value)
        arrays[f"in_{name}"] = v
        args[name] = nc.dram_tensor(f"in_{name}", v.shape, _mybir.dt.from_np(v.dtype), kind="ExternalInput").ap()
    out = nc.dram_tensor("out_0", tuple(given["x"].shape), F32, kind="ExternalOutput").ap()
    adj_preln_d4(nc, args, out)
    r = _run(nc, [arrays], core_ids=[0])
    return r.results[0]["out_0"]
```

```python
from contextlib import ExitStack

import concourse.bass as bass
from concourse import mybir

F32 = mybir.dt.float32
F32R = mybir.dt.float32r
BF16 = mybir.dt.bfloat16
U8 = mybir.dt.uint8
ALU = mybir.AluOpType
ACT = mybir.ActivationFunctionType
AX_X = mybir.AxisListType.X

P = 128
D = 384
NC = D // P
S = 64
GH, GE = 12, 32
MH, ME = 6, 64
GP, MP = GH // 2, MH // 2
EPS = 1e-5
LEAKY = 0.2
PARTS = 3
NOT_ADJ = -999.0
NEG = 9000000000000000.0


def adj_preln_d4(nc: bass.Bass, a, out):
    NT = a["x"].shape[0] // 2
    SLOTS = NT // 2
    x_dram = a["x"].rearrange("(t g) n d -> t (g n) d", g=2)
    adj_dram = a["adj"].rearrange("(t g) n m -> t (g n) m", g=2)
    out_dram = out.rearrange("(t g) n d -> t (g n) d", g=2)

    with ExitStack() as ctx:
        def sb(name, shape, dt=F32):
            return ctx.enter_context(nc.sbuf_tensor(name, shape, dt))

        def psum(name, shape):
            return ctx.enter_context(nc.psum_tensor(name, shape, F32))

        def sem(name):
            return ctx.enter_context(nc.semaphore(name))

        x = sb("x_sb", [P, NT, D])
        adj = sb("adj_sb", [P, NT, S], U8)
        w_landing = sb("w_landing", [P, NC, D])
        w_hi = sb("w_hi", [P, 6, NC, D], F32R)
        w_lo = sb("w_lo", [P, 6, NC, D], F32R)
        ident = sb("ident", [P, P])
        ident_bf = sb("ident_bf", [P, P], BF16)
        row_select = sb("row_select", [P, 2, GH])
        select = sb("select", [P, GH, 2, S], BF16)
        headmask = sb("headmask", [P, NC, GH])
        zeros = sb("zeros", [P, 2, GH])
        minus_half = sb("minus_half", [P, 2])
        w_col = sb("w_col", [P, 2, 2, NC])
        w_sd = sb("w_sd", [P, 2, NC, 2 * GH])
        gat_b = sb("gat_b", [P, 2, GE])
        hb_split = sb("hb_split", [3, 2, D], BF16)
        ones3 = sb("ones3", [3, P], BF16)
        qk_bias = sb("qk_bias", [P, 2, 2, NC])
        stats = sb("stats", [P, 2, 6])
        moments = sb("moments", [P, 2, 2])
        mean_gap = sb("mean_gap", [P, 2])
        gap_sq = sb("gap_sq", [P, 2])
        neg_mean = sb("neg_mean", [P, 2])
        var_part = sb("var_part", [P, 2])
        var_eps = sb("var_eps", [P, 2])
        rstd = sb("rstd", [P, 2])
        ln_shift = sb("ln_shift", [P, 2])
        h = sb("h", [P, 2, D])
        hT_hi = sb("hT_hi", [P, 2 * D], F32R)
        hT_lo = sb("hT_lo", [P, 2 * D], F32R)
        buf_a = sb("buf_a", [P, 2 * D])
        buf_b = sb("buf_b", [P, 2 * D])
        val = sb("val", [P, 2, 396])
        val_pair = sb("val_pair", [P, 2, 2, 396])
        ctxT_hi, ctxT_lo = sb("ctxT_hi", [P, NC, P], F32R), sb("ctxT_lo", [P, NC, P], F32R)
        logit_rest = sb("logit_rest", [P, 2 * GH])
        logit_parts = sb("logit_parts", [P, 2, S], BF16)
        logitT = sb("logitT", [P, P + S], BF16)
        no_edge = sb("no_edge", [P, 2, S], U8)
        att = sb("att", [P, 2, 2 * D])
        att_top = sb("att_top", [P, 2, GH])
        attT = sb("attT", [P, 2 * D])
        rec = sb("rec", [P, 2, GH])
        u = sb("u", [P, 2, D])
        elu = sb("elu", [P, D])
        th, thT = buf_a[:, 0:D], buf_a[:, D:2 * D]
        qT = buf_a[:].rearrange("p (c t) -> p c t", c=NC)
        kT = buf_b[:].rearrange("p (c t) -> p c t", c=NC)
        gate = buf_b[:].rearrange("p (u d) -> p u d", u=2)
        hT4_hi, hT4_lo = (t[:].rearrange("p (u c t) -> p u c t", u=2, c=NC) for t in (hT_hi, hT_lo))
        hT2_hi, hT2_lo = (t[:].rearrange("p (c u t) -> p u c t", u=2, c=NC) for t in (hT_hi, hT_lo))
        part_of = logit_parts[:, :, 0:PARTS * GH].rearrange("p i (t a) -> p i t a", t=PARTS)
        bv, bf = att[:, 0, D:2 * D], att[:, 1, D:2 * D]
        w_second = att[:].rearrange("p u t -> p (u t)")[:, 0:NC * D].rearrange("p (c d) -> p c d", c=NC)
        omg = thT
        mask_add = elu[:, 0:2 * S].rearrange("p (u m) -> p u m", u=2)
        two = lambda v: v.rearrange("p (i d) -> p i d", i=2)
        pair_rows = val_pair[0:3].rearrange("p u g w -> p (u g w)")
        hb_part = [two(v) for v in (pair_rows[:, 0:2 * D], pair_rows[:, 2 * D:4 * D], attT[0:3, :])]
        hb_bf = [two(v.bitcast(BF16)) for v in (buf_b[0:3, 0:D], buf_b[0:3, D:2 * D], elu[0:3, :])]
        hb_rows = u[0:3]

        ps_t = psum("ps_t", [P, 512])
        ps_h = psum("ps_h", [P, 512])
        ps_g = psum("ps_g", [P, 512])
        ps_s = psum("ps_s", [P, 2, 512])
        ps_f = psum("ps_f", [P, 2, 512])
        ps_o = psum("ps_o", [P, 512])
        qk_bank = [ps_g[:, 0:2 * P], ps_f[:, 1, 0:2 * P]]
        minus_999 = ps_s[:, 0, 511:512]

        x_in = [sem("x_in_even"), sem("x_in_odd")]
        const_in = sem("const_in")
        w_in = [sem("w_in_even"), sem("w_in_odd")]
        bvf_in = sem("bvf_in")
        const_made = sem("const_made")
        w_hi_made, w_lo_made = sem("w_hi_made"), sem("w_lo_made")
        layer_set = sem("layer_set")
        stats_done, moments_done, var_parts_done = sem("stats_done"), sem("moments_done"), sem("var_parts_done")
        var_done, rstd_done, shift_done = sem("var_done"), sem("rstd_done"), sem("shift_done")
        h_done = sem("h_done")
        hT_ps_done, hT_hi_done, hT_lo_done = sem("hT_ps_done"), sem("hT_hi_done"), sem("hT_lo_done")
        hproj_done, gate_ps_done = sem("hproj_done"), sem("gate_ps_done")
        tanh_done, thT_ps_done, thT_done = sem("tanh_done"), sem("thT_ps_done"), sem("thT_done")
        logit_ps_done, part_1_done, rest_done = sem("logit_ps_done"), sem("part_1_done"), sem("rest_done")
        part_2_done, part_3_done = sem("part_2_done"), sem("part_3_done")
        logitT_ps_done, logitT_done = sem("logitT_ps_done"), sem("logitT_done")
        val_done = sem("val_done")
        val_pair_in = [sem("val_pair_in_even"), sem("val_pair_in_odd")]
        s_ps_done = sem("s_ps_done")
        mask_done, masking_ready = sem("mask_done"), sem("masking_ready")
        att_scaled_done = sem("att_scaled_done")
        att_sum_done, att_masked_done = sem("att_sum_done"), sem("att_masked_done")
        att_top_done, att_shift_done, att_exp_done = sem("att_top_done"), sem("att_shift_done"), sem("att_exp_done")
        attT_ps_done, attT_done = sem("attT_ps_done"), sem("attT_done")
        out_ps_done, rec_done, u_done = sem("out_ps_done"), sem("rec_done"), sem("u_done")
        relu_done, exp_done, elu_done, gated_done = sem("relu_done"), sem("exp_done"), sem("elu_done"), sem("gated_done")
        gate_tanh_done, omg_done, gate_done = sem("gate_tanh_done"), sem("omg_done"), sem("gate_done")
        kept_h_done, x_kept_done = sem("kept_h_done"), sem("x_kept_done")
        qk_ps_done, qk_done = sem("qk_ps_done"), sem("qk_done")
        ctxT_ps_done, ctxT_hi_done, ctxT_lo_done = sem("ctxT_ps_done"), sem("ctxT_hi_done"), sem("ctxT_lo_done")
        v_ps_done, y_ps_done = sem("v_ps_done"), sem("y_ps_done")
        x_done = sem("x_done")
        out_written = sem("out_written")

        N_CONST = 16 * 9
        AHEAD = 2
        W_SPLIT = (2, 6, 8, 12)
        W_FIRST = (0, 2, 0, 2)
        SPLIT_AT = (1, 3, NT - 2, NT)

        def due(count):
            return not isinstance(count, int) or count > 0

        def there(k):
            return not isinstance(k, int) or 0 <= k < NT

        def ahead_of(layer, j):
            return (layer + 1, j - NT) if isinstance(j, int) and j >= NT else (layer, j)

        def slots(eng, slot):
            for T in range(2):
                slot(T)
            with eng.Fori(2, SLOTS - 1, 1) as T:
                slot(T)
            for T in range(SLOTS - 1, SLOTS + 1):
                slot(T)

        def landing(layer, i):
            return w_second if (layer, i) == (0, 1) else w_landing[:]

        def landed(layer, i):
            if i % 2 == 0:
                return 16 * ((0, NC, NC + 2, 2 * NC + 2)[layer] + (NC if layer % 2 == 0 else i // 2 + 1))
            return 16 * ((0, 1, 3, 4)[layer] + i // 2 + 1)

        QK = ((0, 0), (0, 1), (1, 0), (0, 2), (1, 2), (1, 1))

        block = ctx.enter_context(nc.Block())

        @block.sync
        def _(sp):
            def load_w(layer, i):
                n = (("W", "H_wT"), ("Wq", "Wk", "Wv", "Wf"))[layer % 2][i]
                w = a[f"L{layer}_gnn_{n}"]
                to = landing(layer, i)
                if layer > 0:
                    sp.wait_ge(w_lo_made, (0, *W_SPLIT)[layer] + i)
                    sp.wait_ge(w_hi_made, (0, *W_SPLIT)[layer] + i)
                if n == "W":
                    for c in range(NC):
                        sp.dma_start(to[:, c, :].rearrange("p (a e) -> p a e", a=GH),
                                     w[:, c * P:(c + 1) * P, :].rearrange("a p e -> p a e")).then_inc(w_in[i % 2], 16)
                else:
                    sp.dma_start(to, w.rearrange("(c p) e -> p c e", p=P)).then_inc(w_in[i % 2], 16)

            def load_x(T, par):
                k = 2 * T + par
                if due(need := 32 * T):
                    sp.wait_ge(x_in[par], need)
                sp.dma_start(x[:, k, :], x_dram[k]).then_inc(x_in[par], 16)
                sp.dma_start(adj[:, k, :], adj_dram[k]).then_inc(x_in[par], 16)

            def pair_values(layer, par, count):
                w = 6 * 33 if layer % 2 == 0 else 3 * 65
                sp.wait_ge(val_done, count)
                sp.wait_ge(out_ps_done, count)
                for g in range(2):
                    for half in range(2):
                        sp.dma_start(val_pair[64 * half:64 * half + 64, par, g, half * w:half * w + w],
                                     val[64 * g:64 * g + 64, par, half * w:half * w + w]).then_inc(val_pair_in[par], 16)

            def store_x(T, par):
                k = 2 * T + par
                sp.wait_ge(x_done, 3 * NT + k + 1)
                sp.dma_start(out_dram[k], x[:, k, :]).then_inc(out_written, 16)

            for par in range(2):
                load_x(0, par)
            sp.dma_start(ident[:], a["c_ident"]).then_inc(const_in, 16)
            load_w(0, 0)
            for dst, src in ((row_select[:], a["c_row_select"]), (headmask[:], a["c_headmask"]),
                             (w_col[:], a["w_src_dst"]), (qk_bias[:], a["bq_bk"])):
                sp.dma_start(dst, src).then_inc(const_in, 16)
            for i in range(2):
                g = f"L{2 * i}_gnn_"
                sp.dma_start(gat_b[:, i, :], a[g + "b"].partition_broadcast(P)).then_inc(const_in, 16)
            for i in range(2):
                sp.dma_start(hb_part[0][:, i, :], a[f"L{2 * i}_gnn_H_b"].partition_broadcast(3)).then_inc(const_in, 16)

            load_w(0, 1)
            for par in range(2):
                load_x(1, par)

            for layer in range(4):
                sp.wait_ge(layer_set, 2 * layer + 2)
                if layer < 3:
                    load_w(layer + 1, 0)
                if layer % 2 == 1:
                    for i, n in enumerate(("bv", "bf")):
                        sp.dma_start((bv, bf)[i], a[f"L{layer}_gnn_{n}"].partition_broadcast(P)).then_inc(bvf_in, 16)

                def slot(T, now, before, after, layer=layer):
                    first = layer * NT + 2 * T
                    counts = [first + par + 1 for par in range(2)]
                    if not isinstance(T, int):
                        counts = [nc.sync.snap(c) for c in counts]
                    for par in range(2):
                        if after and layer == 0:
                            load_x(T + 2, par)
                    for par in range(2):
                        if now:
                            pair_values(layer, par, counts[par])
                        if before and layer == 3:
                            store_x(T - 1, par)

                for T in range(2):
                    slot(T, True, T > 0, True)
                    if layer % 2 == 0 or (layer == 1 and T == 1):
                        load_w(layer + 1, T + 1 if layer % 2 == 0 else 1)
                with sp.Fori(2, SLOTS - 2, 1) as T:
                    slot(T, True, True, True)
                for T in range(SLOTS - 2, SLOTS + 1):
                    slot(T, T < SLOTS, True, False)
                    if layer % 2 == 0 and T == SLOTS - 1:
                        load_w(layer + 1, 3)
            sp.wait_ge(out_written, 16 * NT)

        @block.tensor
        def _(pe):
            def three_pass(out_ap, stat_hi, stat_lo, mov_hi, mov_lo, more=False, chunks=range(NC)):
                for c in chunks:
                    for i, (s, m) in enumerate(((stat_hi, mov_hi), (stat_hi, mov_lo), (stat_lo, mov_hi))):
                        mm = nc.tensor.matmul(out_ap, s(c), m(c), start=(c == 0 and i == 0),
                                              stop=(c == NC - 1 and i == 2 and not more))
                return mm

            def w(i, part):
                return lambda c: part[:, i, c, :]

            def h_T(layer, k, par):
                pe.wait_ge(h_done, layer * NT + k + 1)
                for c in range(NC):
                    mm = nc.tensor.transpose(ps_t[:, c * P:(c + 1) * P], h[:, par, c * P:(c + 1) * P], ident[:])
                mm.then_inc(hT_ps_done, 1)

            def gat(layer):
                G0, L0 = layer // 2 * NT, layer * NT

                def project(k, par):
                    pe.wait_ge(hT_lo_done, L0 + (2 if isinstance(k, int) and k == 0 else k + 1))
                    three_pass(ps_h[:, 0:D], lambda c: hT4_hi[:, par, c, :], lambda c: hT4_lo[:, par, c, :],
                               w(0, w_hi), w(0, w_lo)).then_inc(hproj_done, 1)

                def aggregate(k, par, T):
                    pe.wait_ge(val_pair_in[par], 64 * (layer * SLOTS + T))
                    pe.wait_ge(attT_done, L0 + k + 1)
                    vp = val_pair[:, par].rearrange("q g (b p e) -> q g b p e", b=2, p=GP)
                    for g in range(2):
                        for p in range(GP):
                            mm = nc.tensor.matmul(ps_o[64 * g:64 * g + 64, 66 * p:66 * (p + 1)],
                                                  attT[:, p * P + 64 * g:p * P + 64 * g + 64],
                                                  vp[:, g, :, p, :], start=True, stop=True)
                    mm.then_inc(out_ps_done, 1)

                def tanh_T(k):
                    pe.wait_ge(tanh_done, G0 + k + 1)
                    for c in range(NC):
                        mm = nc.tensor.transpose(ps_t[:, c * P:(c + 1) * P], th[:, c * P:(c + 1) * P], ident[:])
                    mm.then_inc(thT_ps_done, 1)

                def gates(k, par, chunks):
                    if isinstance(k, int) and k == 0:
                        pe.wait_ge(const_made, N_MADE)
                        pe.wait_ge(w_lo_made, W_SPLIT[layer])
                    three_pass(ps_g[:, 0:D], lambda c: hT4_hi[:, par, c, :], lambda c: hT4_lo[:, par, c, :],
                               w(1, w_hi), w(1, w_lo), more=True, chunks=chunks)
                    if NC - 1 in chunks:
                        nc.tensor.matmul(ps_g[:, 0:D], ones3[:], hb_split[:, layer // 2, :], start=False,
                                         stop=True).then_inc(gate_ps_done, 1)

                def node_logits(k):
                    pe.wait_ge(thT_done, G0 + k + 1)
                    for c in range(NC):
                        mm = nc.tensor.matmul(ps_t[:, D:D + 2 * GH], thT[:, c * P:(c + 1) * P],
                                              w_sd[:, layer // 2, c, :], start=(c == 0), stop=(c == NC - 1))
                    mm.then_inc(logit_ps_done, 1)

                def logits_T(k):
                    pe.wait_ge(part_3_done, G0 + k + 1)
                    nc.tensor.matmul(ps_h[:, 0:P], logit_parts[:].rearrange("p i r -> p (i r)"), ident_bf[:],
                                     start=True, stop=True)
                    for g in range(2):
                        t = slice(64 * g, 64 * g + 64)
                        mm = nc.tensor.matmul(ps_h[t, P:P + S], logit_parts[t, 1, :], ident_bf[t, t],
                                              start=True, stop=True)
                    mm.then_inc(logitT_ps_done, 1)

                def att_T(k, par):
                    pe.wait_ge(att_exp_done, L0 + k + 1)
                    for p in range(GP):
                        mm = nc.tensor.transpose(ps_f[:, p // 3, p % 3 * P:(p % 3 + 1) * P],
                                                 att[:, par, p * P:(p + 1) * P], ident[:])
                    mm.then_inc(attT_ps_done, 1)

                def pair_logits(k):
                    pe.wait_ge(logitT_done, G0 + k + 1)
                    rows = PARTS * GH
                    for a in range(GH):
                        to = ps_s[:, a // GP, a % GP * S:(a % GP + 1) * S]
                        nc.tensor.matmul(to, logitT[0:rows, 0:P], select[0:rows, a, 0, :], start=True, stop=False)
                        mm = nc.tensor.matmul(to, select[:, a].rearrange("p g m -> p (g m)"), logitT[:, P:P + S],
                                              start=False, stop=True)
                    mm.then_inc(s_ps_done, 1)

                def step(k, par, T):
                    if there(k - 1):
                        logits_T(k - 1)
                    if not isinstance(k, int) or 2 <= k <= NT + 1:
                        if isinstance(k, int) and k == NT + 1:
                            pe.wait_ge(hT_hi_done, L0 + k)
                            pe.wait_ge(hT_lo_done, L0 + k)
                        h_T(*ahead_of(layer, k), par)
                    if there(k - 1):
                        pair_logits(k - 1)
                    if there(k - 2):
                        att_T(k - 2, par)
                    if there(k):
                        project(k, par)
                    if there(k - 2):
                        aggregate(k - 2, par, T)
                    if there(k):
                        tanh_T(k)
                        gates(k, par, (0, 1))
                        node_logits(k)
                        gates(k, par, (2,))

                def slot(T):
                    step(2 * T, 0, T)
                    step(2 * T + 1, 1, T)

                slots(pe, slot)

            def mha(layer):
                M0, L0 = layer // 2 * NT, layer * NT

                def project_T(T, i):
                    if i == 0:
                        pe.wait_ge(hT_lo_done, L0 + 2 * T + 2)
                    if due(need := 3 * M0 + 6 * T + i - 1):
                        pe.wait_ge(qk_done, need)
                    mats, c2 = 2 + QK[i][0], QK[i][1]
                    hi2, lo2 = (t[:].rearrange("p (c t) -> p c t", c=NC) for t in (hT_hi, hT_lo))
                    three_pass(qk_bank[i % 2], lambda c: w_hi[:, mats, c, c2 * P:(c2 + 1) * P],
                               lambda c: w_lo[:, mats, c, c2 * P:(c2 + 1) * P],
                               lambda c: hi2[:, c, :], lambda c: lo2[:, c, :]).then_inc(qk_ps_done, 1)

                def values(k, par):
                    pe.wait_ge(val_done, L0 + k)
                    if par == 0:
                        pe.wait_ge(qk_done, 3 * M0 + 3 * k + 6)
                    else:
                        pe.wait_ge(att_sum_done, M0 + k)
                    three_pass(ps_h[:, 0:D], lambda c: hT2_hi[:, par, c, :], lambda c: hT2_lo[:, par, c, :],
                               w(4, w_hi), w(4, w_lo)).then_inc(v_ps_done, 1)

                def scores(k, par):
                    for b in range(2):
                        for g in range(2):
                            for c in range(NC):
                                t = par * P + 64 * g
                                mm = nc.tensor.matmul(ps_s[64 * g:64 * g + 64, b, c * S:(c + 1) * S],
                                                      qT[64 * b:64 * b + 64, c, t:t + 64],
                                                      kT[64 * b:64 * b + 64, c, t:t + 64], start=True, stop=True)
                    mm.then_inc(s_ps_done, 1)

                def att_T(k, par):
                    pe.wait_ge(att_exp_done, L0 + k + 1)
                    pe.wait_ge(attT_done, L0 + k)
                    for c in range(NC):
                        mm = nc.tensor.transpose(ps_f[:, 0, c * P:(c + 1) * P], att[:, par, c * P:(c + 1) * P], ident[:])
                    mm.then_inc(attT_ps_done, 1)

                def aggregate(T, k, par):
                    pe.wait_ge(attT_done, L0 + k + 1)
                    pe.wait_ge(val_pair_in[par], 64 * (layer * SLOTS + T + 1))
                    if par == 1:
                        pe.wait_ge(u_done, L0 + k)
                    elif due(need := k):
                        pe.wait_ge(x_done, L0 + need)
                    vp = val_pair[:, par, :, 0:390].rearrange("q g (b p e) -> q g b p e", b=2, p=MP)
                    for g in range(2):
                        for c in range(NC):
                            o = par * D + c * P + 64 * g
                            mm = nc.tensor.matmul(ps_o[64 * g:64 * g + 64, 130 * c:130 * (c + 1)],
                                                  attT[:, o:o + 64], vp[:, g, :, c, :], start=True, stop=True)
                    mm.then_inc(out_ps_done, 1)

                def context_T(k, par):
                    pe.wait_ge(u_done, L0 + k + 1)
                    if par == 1:
                        pe.wait_ge(ctxT_lo_done, M0 + k)
                    for c in range(NC):
                        mm = nc.tensor.transpose(ps_t[:, c * P:(c + 1) * P], u[:, par, c * P:(c + 1) * P], ident[:])
                    mm.then_inc(ctxT_ps_done, 1)

                def project_out(k, par):
                    pe.wait_ge(ctxT_lo_done, M0 + k + 1)
                    if par == 0:
                        pe.wait_ge(u_done, L0 + k + 2)
                    else:
                        pe.wait_ge(x_done, L0 + k)
                    three_pass(ps_o[:, 0:D], lambda c: ctxT_hi[:, c, :], lambda c: ctxT_lo[:, c, :],
                               w(5, w_hi), w(5, w_lo)).then_inc(y_ps_done, 1)

                def slot(T):
                    s0, s1, p0, p1 = 2 * T, 2 * T + 1, 2 * T - 2, 2 * T - 1
                    now, before, after = there(s0), there(p0), there(s0) and (layer < 3 or there(s0 + 2))
                    if now:
                        project_T(T, 0)
                    if before:
                        att_T(p1, 1)
                    if now:
                        project_T(T, 1)
                    if before:
                        aggregate(T - 1, p0, 0)
                    if now:
                        for i in (2, 3, 4):
                            project_T(T, i)
                    if before:
                        context_T(p0, 0)
                    if now:
                        project_T(T, 5)
                    if before:
                        aggregate(T - 1, p1, 1)
                    if now:
                        values(s0, 0)
                        scores(s0, 0)
                    if before:
                        context_T(p1, 1)
                        project_out(p0, 0)
                    if now:
                        values(s1, 1)
                    if after:
                        if before:
                            pe.wait_ge(ctxT_lo_done, M0 + p1 + 1)
                        h_T(*ahead_of(layer, s0 + 2), 0)
                    if now:
                        scores(s1, 1)
                        att_T(s0, 0)
                    if after:
                        pe.wait_ge(hT_lo_done, L0 + s0 + 3)
                        h_T(*ahead_of(layer, s1 + 2), 1)
                    if before:
                        project_out(p1, 1)

                slots(pe, slot)

            pe.wait_ge(const_in, N_CONST)
            for par in range(2):
                if par > 0:
                    pe.wait_ge(hT_hi_done, 1)
                    pe.wait_ge(hT_lo_done, 1)
                h_T(0, par, par)
            pe.wait_ge(const_made, MADE_FIRST)
            for layer in range(4):
                if layer > 0:
                    pe.wait_ge(x_done, layer * NT)
                pe.wait_ge(w_lo_made, W_SPLIT[layer] - (1 if layer % 2 == 0 else 0))
                (gat if layer % 2 == 0 else mha)(layer)

        @block.scalar
        def _(act):
            def norm_relu(layer, k, par, T, free=True):
                if not free and due(need := layer * NT + k - 1):
                    act.wait_ge(x_kept_done, need)
                act.wait_ge(shift_done, layer * SLOTS + T + 1)
                nc.scalar.activation(h[:, par, :], x[:, k, :], ACT.Relu, bias=ln_shift[:, par:par + 1],
                                     scale=rstd[:, par:par + 1]).then_inc(h_done, 1)

            def hT_part(layer, k, par):
                act.wait_ge(hT_ps_done, layer * NT + k + 1)
                dst = (hT4_hi if layer % 2 == 0 else hT2_hi)[:, par]
                nc.scalar.activation(dst, ps_t[:, 0:D].rearrange("p (c t) -> p c t", c=NC),
                                     ACT.Copy).then_inc(hT_hi_done, 1)

            def weights_hi(layer, i):
                act.wait_ge(w_in[i % 2], landed(layer, i))
                nc.scalar.activation(w_hi[:, W_FIRST[layer] + i], landing(layer, i), ACT.Copy).then_inc(w_hi_made, 1)

            def att_exp(layer, k, par, n):
                act.wait_ge(att_shift_done, layer * NT + k + 1)
                nc.scalar.activation(att[:, par, 0:n], att[:, par, 0:n], ACT.Exp).then_inc(att_exp_done, 1)

            def gat(layer):
                G0, L0 = layer // 2 * NT, layer * NT

                def tanh(k):
                    act.wait_ge(hproj_done, G0 + k + 1)
                    nc.scalar.activation(th, ps_h[:, 0:D], ACT.Tanh).then_inc(tanh_done, 1)

                def thT_copy(k):
                    if due(need := G0 + k):
                        act.wait_ge(kept_h_done, need)
                    act.wait_ge(thT_ps_done, G0 + k + 1)
                    nc.scalar.activation(thT, ps_t[:, 0:D], ACT.Copy).then_inc(thT_done, 1)

                def att_scaled(k, par):
                    act.wait_ge(s_ps_done, L0 + k + 1)
                    nc.scalar.activation(att[:, par, :].rearrange("p (b t) -> p b t", b=2), ps_s[:, :, 0:D],
                                         ACT.Copy, scale=LEAKY).then_inc(att_scaled_done, 1)

                def logitT_copy(k):
                    act.wait_ge(logitT_ps_done, G0 + k + 1)
                    nc.scalar.activation(logitT[:], ps_h[:, 0:P + S], ACT.Copy).then_inc(logitT_done, 1)

                def attT_copy(k):
                    act.wait_ge(attT_ps_done, L0 + k + 1)
                    nc.scalar.activation(attT[:].rearrange("p (b t) -> p b t", b=2), ps_f[:, :, 0:D],
                                         ACT.Copy).then_inc(attT_done, 1)

                def elu_exp(k, par):
                    e = elu[:]
                    act.wait_ge(u_done, L0 + k + 1)
                    nc.scalar.activation(e, u[:, par, :], ACT.Relu, scale=-1.0).then_inc(relu_done, 1)
                    act.wait_ge(relu_done, G0 + k + 1)
                    nc.scalar.activation(e, e, ACT.Exp, scale=-1.0).then_inc(exp_done, 1)

                def gate_tanh(k, par):
                    act.wait_ge(gate_ps_done, G0 + k + 1)
                    if due(need := G0 + k - 1):
                        act.wait_ge(gated_done, need)
                    nc.scalar.activation(gate[:, par, :], ps_g[:, 0:D], ACT.Tanh, scale=0.5).then_inc(gate_tanh_done, 1)

                def gate_rest(k, par):
                    act.wait_ge(gate_tanh_done, G0 + k + 1)
                    nc.scalar.activation(omg, gate[:, par, :], ACT.Copy, scale=-0.5, bias=0.5).then_inc(omg_done, 1)

                def gate_scale(k, par):
                    act.wait_ge(omg_done, G0 + k + 1)
                    nc.scalar.activation(gate[:, par, :], gate[:, par, :], ACT.Copy, scale=0.5,
                                         bias=0.5).then_inc(gate_done, 1)

                def step(k, par, T):
                    if there(k):
                        tanh(k)
                        thT_copy(k)
                    after = not isinstance(k, int) or 0 < k <= NT
                    nl, nk = ahead_of(layer, k + 1)
                    if after:
                        norm_relu(nl, nk, 1 - par, 0 if nl > layer else T + par, free=False)
                    if there(k - 2):
                        elu_exp(k - 2, par)
                    if there(k - 1):
                        att_exp(layer, k - 1, 1 - par, 2 * D)
                    if there(k):
                        logitT_copy(k)
                    if after:
                        hT_part(nl, nk, 1 - par)
                    if there(k):
                        gate_tanh(k, par)
                        att_scaled(k, par)
                        gate_rest(k, par)
                    if there(k - 1):
                        attT_copy(k - 1)
                    if there(k):
                        gate_scale(k, par)
                    if isinstance(k, int) and k in SPLIT_AT:
                        weights_hi(layer + 1, SPLIT_AT.index(k))

                def slot(T):
                    step(2 * T, 0, T)
                    step(2 * T + 1, 1, T)

                slots(act, slot)

            def mha(layer):
                M0, L0 = layer // 2 * NT, layer * NT

                def qk_copy(T, i):
                    act.wait_ge(qk_ps_done, 3 * M0 + 6 * T + i + 1)
                    if i == 0:
                        act.wait_ge(s_ps_done, L0 + 2 * T)
                    m, c = QK[i]
                    nc.scalar.activation((qT, kT)[m][:, c, :], qk_bank[i % 2], ACT.Identity,
                                         bias=qk_bias[:, layer // 2, m, c:c + 1],
                                         scale=ME ** -0.5 if m == 0 else 1.0).then_inc(qk_done, 1)

                def attT_copy(k, par):
                    act.wait_ge(attT_ps_done, L0 + k + 1)
                    act.wait_ge(out_ps_done, AHEAD + L0 + k - 1)
                    nc.scalar.activation(attT[:, par * D:(par + 1) * D], ps_f[:, 0, 0:D], ACT.Copy).then_inc(attT_done, 1)

                def context_hi(k):
                    act.wait_ge(ctxT_ps_done, M0 + k + 1)
                    if due(need := M0 + k):
                        act.wait_ge(y_ps_done, need)
                    nc.scalar.activation(ctxT_hi[:], ps_t[:, 0:D].rearrange("p (c t) -> p c t", c=NC),
                                         ACT.Copy).then_inc(ctxT_hi_done, 1)

                def slot(T):
                    s0, s1, p0, p1 = 2 * T, 2 * T + 1, 2 * T - 2, 2 * T - 1
                    now, before, after = there(s0), there(p0), there(s0) and (layer < 3 or there(s0 + 2))
                    (nl, n0), (_, n1) = ahead_of(layer, s0 + 2), ahead_of(layer, s1 + 2)
                    nT = 0 if nl > layer else T + 1
                    if now:
                        qk_copy(T, 0)
                        qk_copy(T, 1)
                    if before:
                        attT_copy(p1, 1)
                    if now:
                        qk_copy(T, 2)
                        qk_copy(T, 3)
                    if before:
                        context_hi(p0)
                    if now:
                        qk_copy(T, 4)
                        qk_copy(T, 5)
                    if after:
                        norm_relu(nl, n0, 0, nT)
                    if before:
                        context_hi(p1)
                    if after:
                        norm_relu(nl, n1, 1, nT)
                    if now:
                        att_exp(layer, s0, 0, D)
                    if after:
                        hT_part(nl, n0, 0)
                    if now:
                        attT_copy(s0, 0)
                    if after:
                        hT_part(nl, n1, 1)
                    if now:
                        att_exp(layer, s1, 1, D)
                    if layer < 3 and isinstance(T, int) and T in (1, SLOTS - 1):
                        weights_hi(layer + 1, 0 if T == 1 else 1)

                slots(act, slot)

            nc.scalar.preload_act_table(ACT.Exp)
            norm_relu(0, 0, 0, 0)
            norm_relu(0, 1, 1, 0)
            hT_part(0, 0, 0)
            hT_part(0, 1, 1)
            weights_hi(0, 0)
            weights_hi(0, 1)
            for layer in range(4):
                if layer > 0:
                    act.wait_ge(x_done, layer * NT)
                (gat if layer % 2 == 0 else mha)(layer)

        @block.vector
        def _(dve):
            def row_stats(layer, T, pars=(0, 1)):
                if layer > 0 and isinstance(T, int) and T == 0 and 0 in pars:
                    dve.wait_ge(x_done, (layer - 1) * NT + 2)
                for par in pars:
                    if layer == 0:
                        dve.wait_ge(x_in[par], 32 * (T + 1))
                    nc.vector.bn_stats(stats[:, par, :], x[:, 2 * T + par, :]).then_inc(stats_done, 1)

            def halves(layer, T):
                n = layer * SLOTS + T
                dve.wait_ge(stats_done, 2 * n + 2)
                nc.vector.tensor_tensor(moments[:], stats[:, :, 1:3], stats[:, :, 4:6], ALU.add).then_inc(moments_done, 1)
                nc.vector.tensor_tensor(mean_gap[:], stats[:, :, 1], stats[:, :, 4], ALU.subtract).then_inc(moments_done, 1)

            def variance_parts(layer, T):
                n = layer * SLOTS + T
                dve.wait_ge(moments_done, 2 * n + 2)
                if due(need := n):
                    dve.wait_ge(shift_done, need)
                nc.vector.scalar_tensor_tensor(out=gap_sq[:], in0=mean_gap[:], scalar=0.25, in1=mean_gap[:],
                                               op0=ALU.mult, op1=ALU.mult).then_inc(var_parts_done, 1)
                nc.vector.tensor_scalar(var_part[:], moments[:, :, 1], 1.0 / D, EPS, ALU.mult, ALU.add).then_inc(var_parts_done, 1)
                nc.vector.tensor_scalar(neg_mean[:], moments[:, :, 0], -0.5, None, ALU.mult).then_inc(var_parts_done, 1)

            def variance(layer, T):
                dve.wait_ge(var_parts_done, 3 * (layer * SLOTS + T) + 3)
                nc.vector.tensor_tensor(var_eps[:], var_part[:], gap_sq[:], ALU.add).then_inc(var_done, 1)

            def coefficients(layer, T):
                row_stats(layer, T)
                halves(layer, T)
                variance_parts(layer, T)
                variance(layer, T)

            def hT_part(layer, k, par):
                dve.wait_ge(hT_hi_done, layer * NT + k + 1)
                dst, hi = ((hT4_lo, hT4_hi) if layer % 2 == 0 else (hT2_lo, hT2_hi))
                nc.vector.tensor_tensor(dst[:, par], ps_t[:, 0:D].rearrange("p (c t) -> p c t", c=NC),
                                        hi[:, par].bitcast(F32), ALU.subtract).then_inc(hT_lo_done, 1)

            def att_max(layer, k, par, nh):
                nc.vector.tensor_reduce(att_top[:, par, 0:nh], att[:, par, 0:nh * S].rearrange("p (a m) -> p a m", a=nh),
                                        AX_X, ALU.max).then_inc(att_top_done, 1)

            def gat(layer):
                G0, L0 = layer // 2 * NT, layer * NT

                def add_bias(k, par, T):
                    dve.wait_ge(tanh_done, G0 + k + 1)
                    v = val[:, par, :].rearrange("q (b p e) -> q p b e", b=2, p=GP)
                    nc.vector.tensor_tensor(v[:, :, :, 0:GE], ps_h[:, 0:D].rearrange("q (p b e) -> q p b e", p=GP, b=2),
                                            gat_b[:, layer // 2, :].unsqueeze(1).unsqueeze(1).broadcast_to([P, GP, 2, GE]),
                                            ALU.add).then_inc(val_done, 1)

                def mask(k, par):
                    nc.vector.tensor_scalar(no_edge[:, par, :], adj[:, k, :], 0.0, None, ALU.is_equal).then_inc(masking_ready, 1)

                def logits(k):
                    dve.wait_ge(logit_ps_done, G0 + k + 1)
                    if due(need := G0 + k):
                        dve.wait_ge(logitT_ps_done, need)
                    src_dst = ps_t[:, D:D + 2 * GH].rearrange("p (i a) -> p i a", i=2)
                    nc.vector.tensor_copy(part_of[:, :, 0, :], src_dst).then_inc(part_1_done, 1)
                    dve.wait_ge(part_1_done, G0 + k + 1)
                    nc.vector.tensor_tensor(logit_rest[:].rearrange("p (i a) -> p i a", i=2), src_dst,
                                            part_of[:, :, 0, :], ALU.subtract).then_inc(rest_done, 1)

                def att_leaky(k, par):
                    dve.wait_ge(att_scaled_done, G0 + k + 1)
                    v = att[:, par, :].rearrange("p (b t) -> p b t", b=2)
                    nc.vector.tensor_tensor(v, ps_s[:, :, 0:D], v, ALU.max).then_inc(masking_ready, 1)

                def att_masked(k, par):
                    a3 = att[:, par, :].rearrange("p (a m) -> p a m", a=GH)
                    nc.vector.copy_predicated(a3, no_edge[:, par, :].unsqueeze(1).broadcast_to([P, GH, S]),
                                              minus_999.unsqueeze(2).broadcast_to([P, GH, S])).then_inc(att_masked_done, 1)
                def inverse_sums(k, par):
                    dve.wait_ge(out_ps_done, AHEAD + L0 + k + 1)
                    nc.vector.reciprocal(rec[:, par, :], ps_o[:, 0:GH * 33].rearrange("p (a e) -> p a e", a=GH)[:, :, GE]
                                         ).then_inc(rec_done, 1)

                def normalise(k, par):
                    dve.wait_ge(rec_done, L0 + k + 1)
                    v = ps_o[:, 0:GH * 33].rearrange("p (a e) -> p a e", a=GH)
                    nc.vector.tensor_tensor(u[:, par, :].rearrange("p (a e) -> p a e", a=GH), v[:, :, 0:GE],
                                            rec[:, par, :].unsqueeze(2).broadcast_to([P, GH, GE]), ALU.mult).then_inc(u_done, 1)

                def gated(k, par):
                    dve.wait_ge(exp_done, G0 + k + 1)
                    nc.vector.scalar_tensor_tensor(out=u[:, par, :], in0=u[:, par, :], scalar=0.0,
                                                   in1=elu[:], op0=ALU.max,
                                                   op1=ALU.add).then_inc(elu_done, 1)
                    dve.wait_ge(elu_done, G0 + k + 1)
                    nc.vector.scalar_tensor_tensor(out=u[:, par, :], in0=u[:, par, :], scalar=-1.0,
                                                   in1=gate[:, par, :], op0=ALU.add, op1=ALU.mult).then_inc(gated_done, 1)

                def step(k, par, T):
                    if there(k - 1):
                        dve.wait_ge(att_masked_done, G0 + k)
                        att_max(layer, k - 1, 1 - par, GH)
                    if there(k - 2):
                        inverse_sums(k - 2, par)
                        normalise(k - 2, par)
                    if there(k):
                        add_bias(k, par, T)
                        logits(k)
                    coef = par == 0 and (not isinstance(T, int) or T < SLOTS)
                    if coef:
                        nl, nk = ahead_of(layer, k + 2)
                        nT = 0 if nl > layer else T + 1
                        row_stats(nl, nT, (0,))
                    if there(k - 2):
                        gated(k - 2, par)
                    if coef:
                        row_stats(nl, nT, (1,))
                    if not isinstance(k, int) or 0 < k <= NT:
                        hT_part(*ahead_of(layer, k + 1), 1 - par)
                    if coef:
                        halves(nl, nT)
                        variance_parts(nl, nT)
                        variance(nl, nT)
                    if isinstance(k, int) and k == 0:
                        mask(0, 0)
                    if there(k):
                        att_leaky(k, par)
                    if there(k):
                        dve.wait_ge(masking_ready, 2 * (G0 + k + 1))
                        if there(k + 1):
                            mask(k + 1, 1 - par)
                        att_masked(k, par)
                    if isinstance(k, int) and k in SPLIT_AT:
                        weights_lo(layer + 1, SPLIT_AT.index(k))

                def slot(T):
                    step(2 * T, 0, T)
                    step(2 * T + 1, 1, T)

                slots(dve, slot)

            def weights_lo(layer, i):
                j = W_FIRST[layer] + i
                dve.wait_ge(w_hi_made, (0, *W_SPLIT)[layer] + i + 1)
                nc.vector.tensor_tensor(w_lo[:, j], landing(layer, i), w_hi[:, j].bitcast(F32),
                                        ALU.subtract).then_inc(w_lo_made, 1)

            def mha(layer):
                M0, L0 = layer // 2 * NT, layer * NT

                def add_bias(k, par, T):
                    dve.wait_ge(v_ps_done, M0 + k + 1)
                    dve.wait_ge(val_pair_in[par], 64 * (layer * SLOTS + T))
                    v = val[:, par, 0:390].rearrange("q (b c e) -> q c b e", b=2, c=MP)
                    nc.vector.tensor_tensor(v[:, :, :, 0:ME], ps_h[:, 0:D].rearrange("q (c b e) -> q c b e", c=MP, b=2),
                                            bv.rearrange("q (c b e) -> q c b e", c=MP, b=2), ALU.add).then_inc(val_done, 1)

                def mask(k, par):
                    if due(need := M0 + k - 1):
                        dve.wait_ge(att_sum_done, need)
                    nc.vector.tensor_scalar(mask_add[:, par, :], adj[:, k, :], -1.0, NEG, ALU.add, ALU.mult).then_inc(mask_done, 1)

                def att_logits(k, par):
                    dve.wait_ge(s_ps_done, L0 + k + 1)
                    dve.wait_ge(attT_ps_done, L0 + k - 1)
                    dve.wait_ge(mask_done, M0 + k + 1)
                    nc.vector.tensor_tensor(att[:, par, 0:D].rearrange("p (c b m) -> p b c m", b=2, c=MP),
                                            ps_s[:, :, 0:MP * S].rearrange("p b (c m) -> p b c m", c=MP),
                                            mask_add[:, par, :].unsqueeze(1).unsqueeze(1).broadcast_to([P, 2, MP, S]),
                                            ALU.add).then_inc(att_sum_done, 1)

                def inverse_sums(k, par):
                    dve.wait_ge(out_ps_done, AHEAD + L0 + k + 1)
                    nc.vector.reciprocal(rec[:, par, 0:MH], ps_o[:, 0:390].rearrange("p (a e) -> p a e", a=MH)[:, :, ME]
                                         ).then_inc(rec_done, 1)

                def normalise(k, par):
                    dve.wait_ge(rec_done, L0 + k + 1)
                    v = ps_o[:, 0:390].rearrange("p (a e) -> p a e", a=MH)
                    nc.vector.tensor_tensor(u[:, par, :].rearrange("p (a e) -> p a e", a=MH), v[:, :, 0:ME],
                                            rec[:, par, 0:MH].unsqueeze(2).broadcast_to([P, MH, ME]), ALU.mult).then_inc(u_done, 1)

                def context_lo(k):
                    dve.wait_ge(ctxT_hi_done, M0 + k + 1)
                    nc.vector.tensor_tensor(ctxT_lo[:], ps_t[:, 0:D].rearrange("p (c t) -> p c t", c=NC),
                                            ctxT_hi[:].bitcast(F32), ALU.subtract).then_inc(ctxT_lo_done, 1)

                def finish(k):
                    dve.wait_ge(y_ps_done, M0 + k + 1)
                    dve.wait_ge(x_kept_done, L0 + k + 1)
                    nc.vector.tensor_tensor(x[:, k, :], ps_o[:, 0:D], x[:, k, :], ALU.add).then_inc(x_done, 1)

                def slot(T):
                    s0, s1, p0, p1 = 2 * T, 2 * T + 1, 2 * T - 2, 2 * T - 1
                    now, before, after = there(s0), there(p0), there(s0) and (layer < 3 or there(s0 + 2))
                    (nl, n0), (_, n1) = ahead_of(layer, s0 + 2), ahead_of(layer, s1 + 2)
                    nT = 0 if nl > layer else T + 1
                    if before:
                        inverse_sums(p0, 0)
                        normalise(p0, 0)
                    if now:
                        mask(s0, 0)
                        mask(s1, 1)
                    if after:
                        row_stats(nl, nT)
                    if before:
                        inverse_sums(p1, 1)
                    if after:
                        halves(nl, nT)
                    if before:
                        context_lo(p0)
                    if after:
                        variance_parts(nl, nT)
                    if before:
                        normalise(p1, 1)
                    if after:
                        variance(nl, nT)
                    if now:
                        att_logits(s0, 0)
                        add_bias(s0, 0, T)
                        dve.wait_ge(att_sum_done, M0 + s0 + 1)
                        att_max(layer, s0, 0, MH)
                    if before:
                        finish(p0)
                        context_lo(p1)
                    if after:
                        hT_part(nl, n0, 0)
                    if now:
                        att_logits(s1, 1)
                        add_bias(s1, 1, T)
                        dve.wait_ge(att_sum_done, M0 + s1 + 1)
                        att_max(layer, s1, 1, MH)
                    if after:
                        hT_part(nl, n1, 1)
                    if before:
                        finish(p1)
                    if layer < 3 and isinstance(T, int) and T in (1, SLOTS - 1):
                        weights_lo(layer + 1, 0 if T == 1 else 1)

                slots(dve, slot)

            nc.vector.memset(minus_half[:], -0.5).then_inc(const_made, 1)
            coefficients(0, 0)
            dve.wait_ge(const_in, N_CONST)
            nc.vector.memset(zeros[:], 0.0).then_inc(out_ps_done, AHEAD)
            nc.vector.memset(minus_999, NOT_ADJ).then_inc(const_made, 1)
            nc.vector.memset(ones3[:], 1.0).then_inc(const_made, 1)
            nc.vector.memset(logit_parts[:], 0.0).then_inc(const_made, 1)
            nc.vector.tensor_copy(ident_bf[:], ident[:]).then_inc(const_made, 1)
            nc.vector.tensor_copy(select[:], row_select[:].rearrange("p g a -> p a g").unsqueeze(3).broadcast_to([P, GH, 2, S])).then_inc(const_made, 1)
            for i in range(2):
                for j in range(2):
                    nc.vector.tensor_tensor(w_sd[:, i, :, j * GH:(j + 1) * GH], headmask[:],
                                            w_col[:, i, j, :].unsqueeze(2).broadcast_to([P, NC, GH]),
                                            ALU.mult).then_inc(const_made, 1)
                nc.vector.tensor_scalar(qk_bias[:, i, 0, :], qk_bias[:, i, 0, :], ME ** -0.5, None, ALU.mult).then_inc(const_made, 1)
            hT_part(0, 0, 0)
            weights_lo(0, 0)
            hT_part(0, 1, 1)
            made = MADE_FIRST
            for i in range(3):
                nc.vector.tensor_copy(hb_bf[i], hb_part[i]).then_inc(const_made, 1)
                made += 1
                dve.wait_ge(const_made, made)
                if i < 2:
                    nc.vector.tensor_tensor(hb_part[i + 1], hb_part[i], hb_bf[i], ALU.subtract).then_inc(const_made, 1)
                    made += 1
                    dve.wait_ge(const_made, made)
            nc.vector.tensor_scalar(hb_rows, hb_bf[0], ident[0:3, 0:1], None, ALU.mult).then_inc(const_made, 1)
            made += 1
            dve.wait_ge(const_made, made)
            nc.vector.scalar_tensor_tensor(out=hb_rows, in0=hb_bf[1], scalar=ident[0:3, 1:2], in1=hb_rows,
                                           op0=ALU.mult, op1=ALU.add).then_inc(const_made, 1)
            made += 1
            dve.wait_ge(const_made, made)
            nc.vector.scalar_tensor_tensor(out=hb_split[:], in0=hb_bf[2], scalar=ident[0:3, 2:3], in1=hb_rows,
                                           op0=ALU.mult, op1=ALU.add).then_inc(const_made, 1)
            made += 1
            assert made == N_MADE
            weights_lo(0, 1)
            for layer in range(4):
                if layer > 0:
                    dve.wait_ge(x_done, layer * NT)
                dve.wait_ge(layer_set, 2 * layer + 1)
                if layer % 2 == 1:
                    dve.wait_ge(bvf_in, 32 * (layer // 2 + 1))
                (gat if layer % 2 == 0 else mha)(layer)

        @block.gpsimd
        def _(pool):
            def coefficients(layer, T):
                n = layer * SLOTS + T
                pool.wait_ge(var_done, n + 1)
                if due(need := 2 * n):
                    pool.wait_ge(h_done, need)
                nc.gpsimd.tensor_tensor(rstd[:], var_eps[:], minus_half[:], ALU.pow).then_inc(rstd_done, 1)
                pool.wait_ge(rstd_done, n + 1)
                nc.gpsimd.tensor_tensor(ln_shift[:], neg_mean[:], rstd[:], ALU.mult).then_inc(shift_done, 1)

            def shift(layer, k, par, nh):
                pool.wait_ge(att_top_done, layer * NT + k + 1)
                v = att[:, par, 0:nh * S].rearrange("p (a m) -> p a m", a=nh)
                nc.gpsimd.tensor_tensor(v, v, att_top[:, par, 0:nh].unsqueeze(2).broadcast_to([P, nh, S]),
                                        ALU.subtract).then_inc(att_shift_done, 1)

            def gat(layer):
                G0, L0 = layer // 2 * NT, layer * NT

                def keep_h(k, par):
                    pool.wait_ge(omg_done, G0 + k + 1)
                    nc.gpsimd.tensor_tensor(h[:, par, :], h[:, par, :], omg, ALU.mult).then_inc(kept_h_done, 1)

                def keep_x(k, par):
                    pool.wait_ge(kept_h_done, G0 + k + 1)
                    nc.gpsimd.tensor_tensor(x[:, k, :], x[:, k, :], h[:, par, :], ALU.add).then_inc(x_kept_done, 1)

                def parts(k):
                    pool.wait_ge(rest_done, G0 + k + 1)
                    rest = logit_rest[:].rearrange("p (i a) -> p i a", i=2)
                    nc.gpsimd.tensor_tensor(part_of[:, :, 1, :], rest, zeros[:], ALU.add).then_inc(part_2_done, 1)
                    pool.wait_ge(part_2_done, G0 + k + 1)
                    nc.gpsimd.tensor_tensor(part_of[:, :, 2, :], rest, part_of[:, :, 1, :],
                                            ALU.subtract).then_inc(part_3_done, 1)

                def finish(k, par, half):
                    pool.wait_ge(gated_done, G0 + k + 1)
                    xk = x[:].rearrange("p (t s) d -> p t s d", s=2)[:, half, par, :]
                    nc.gpsimd.tensor_tensor(xk, xk, u[:, par, :], ALU.add).then_inc(x_done, 1)

                def step(k, par, T):
                    if there(k - 1):
                        keep_h(k - 1, 1 - par)
                    if there(k - 1):
                        keep_x(k - 1, 1 - par)
                        shift(layer, k - 1, 1 - par, GH)
                    if there(k - 2):
                        pool.wait_ge(x_kept_done, L0 + k - 1)
                    if there(k):
                        parts(k)
                    if there(k - 2):
                        finish(k - 2, par, T - 1)
                    if par == 0 and (not isinstance(T, int) or T < SLOTS):
                        nl, nk = ahead_of(layer, k + 2)
                        coefficients(nl, 0 if nl > layer else T + 1)

                def slot(T):
                    step(2 * T, 0, T)
                    step(2 * T + 1, 1, T)

                slots(pool, slot)

            def mha(layer):
                def add_bf(k):
                    pool.wait_ge(h_done, layer * NT + k + 1)
                    nc.gpsimd.tensor_tensor(x[:, k, :], x[:, k, :], bf, ALU.add).then_inc(x_kept_done, 1)

                def slot(T):
                    s0, s1 = 2 * T, 2 * T + 1
                    if there(s0) and (layer < 3 or there(s0 + 2)):
                        nl, _ = ahead_of(layer, s0 + 2)
                        coefficients(nl, 0 if nl > layer else T + 1)
                    if there(s0):
                        shift(layer, s0, 0, MH)
                        add_bf(s0)
                        add_bf(s1)
                        shift(layer, s1, 1, MH)

                slots(pool, slot)

            pool.wait_ge(const_made, 1)
            coefficients(0, 0)
            for layer in range(4):
                if layer > 0:
                    pool.wait_ge(x_done, layer * NT)
                nc.gpsimd.memset(val[:], 1.0).then_inc(layer_set, 1)
                if layer == 0:
                    pool.wait_ge(const_made, N_MADE)
                nc.gpsimd.memset(val_pair[:], 0.0).then_inc(layer_set, 1)
                if layer % 2 == 1:
                    pool.wait_ge(bvf_in, 32 * (layer // 2 + 1))
                (gat if layer % 2 == 0 else mha)(layer)


MADE_FIRST = 12
N_MADE = MADE_FIRST + 5 + 3


_GAT = ['W', 'b', 'w_src', 'w_dst', 'H_w', 'H_b']
_MHA = ['Wq', 'bq', 'Wk', 'bk', 'Wv', 'bv', 'Wf', 'bf']


def kernel(**inputs):
    import numpy as _np
    import concourse.bacc as _bacc
    from concourse import mybir as _mybir
    from concourse.bass_utils import run_bass_kernel_spmd as _run

    nc = _bacc.Bacc("TRN2", target_bir_lowering=False, num_devices=1)
    given = {"x": inputs["x"], "adj": inputs["adj"]}
    for layer in range(4):
        for n in (_GAT, _MHA)[layer % 2]:
            given[f"L{layer}_gnn_{n}"] = inputs[f"L{layer}_gnn_{n}"]
        if layer % 2 == 0:
            given[f"L{layer}_gnn_H_wT"] = _np.asarray(given.pop(f"L{layer}_gnn_H_w")).T
    for name, of in (("w_src_dst", ("L{}_gnn_w_src", "L{}_gnn_w_dst")), ("bq_bk", ("L{}_gnn_bq", "L{}_gnn_bk"))):
        first = 0 if name == "w_src_dst" else 1
        cols = [[_np.asarray(given.pop(n.format(layer))).reshape(NC, P) for n in of] for layer in (first, first + 2)]
        given[name] = _np.stack([_np.stack(c) for c in cols]).transpose(3, 0, 1, 2)
    given["c_ident"] = _np.eye(P, dtype=_np.float32)
    c = _np.zeros((2, S, 2, GH), dtype=_np.float32)
    for g in range(2):
        c[g, :PARTS * GH, g] = _np.tile(_np.eye(GH), (PARTS, 1))
    given["c_row_select"] = c.reshape(P, 2, GH)
    feature = _np.arange(D).reshape(NC, P).T
    given["c_headmask"] = (feature[:, :, None] // GE == _np.arange(GH)[None, None, :]).astype(_np.float32)
    arrays, args = {}, {}
    for name, value in given.items():
        v = _np.ascontiguousarray(value)
        arrays[f"in_{name}"] = v
        args[name] = nc.dram_tensor(f"in_{name}", v.shape, _mybir.dt.from_np(v.dtype), kind="ExternalInput").ap()
    out = nc.dram_tensor("out_0", tuple(given["x"].shape), F32, kind="ExternalOutput").ap()
    adj_preln_d4(nc, args, out)
    r = _run(nc, [arrays], core_ids=[0])
    return r.results[0]["out_0"]
```
